# Optimizing a Trainium2 kernel written in Bass

```python
import numpy as np
import jax
import jax.numpy as jnp

def _softmax(x, axis=-1):
    return jax.nn.softmax(x, axis=axis)

def _gelu(x):
    return jax.nn.gelu(x, approximate=True)

def _silu(x):
    return jax.nn.silu(x)

def _sigmoid(x):
    return jax.nn.sigmoid(x)

def _layernorm(x, axis=-1, eps=1e-05):
    m = jnp.mean(x, axis=axis, keepdims=True)
    v = jnp.var(x, axis=axis, keepdims=True)
    return (x - m) / jnp.sqrt(v + eps)

def _scatter_add(tgt, idx, src, axis=0):
    return tgt.at[idx].add(src)

def _segment_sum(src, seg, n):
    return jax.ops.segment_sum(src, seg, n)
kernel_name = 'mk_gnn_preln_d2_gnn_r32_dd2c4c'

def setup_inputs(seed: int=0):
    np.random.seed(seed)
    _w = jnp.asarray

    def _rec_inputs():
        import jax
        import jax.numpy as jnp
        _gk = jax.random.key(seed)
        x = -6.415e-05 + 1 * jax.random.normal(jax.random.fold_in(_gk, 1), (625, 512), jnp.float32)
        src = jax.random.randint(jax.random.fold_in(_gk, 2), (10000,), 0, 625, jnp.int32)
        dst = jax.random.randint(jax.random.fold_in(_gk, 3), (10000,), 0, 625, jnp.int32)
        _o = jnp.argsort(dst, stable=True)
        src = src[_o]
        dst = dst[_o]
        edge_attr_20 = jax.random.uniform(jax.random.fold_in(_gk, 12), (10000, 20), jnp.float32, 0.0, 0.999999)
        edge_attr_3 = -0.0005747 + 0.998114 * jax.random.normal(jax.random.fold_in(_gk, 13), (10000, 3), jnp.float32)
        edge_attr_8 = -0.000521468 + 0.999954 * jax.random.normal(jax.random.fold_in(_gk, 14), (10000, 8), jnp.float32)
        edge_attr_8_n2 = -0.000521468 + 0.999954 * jax.random.normal(jax.random.fold_in(_gk, 15), (10000, 8), jnp.float32)
        edge_weight = jax.random.uniform(jax.random.fold_in(_gk, 16), (10000,), jnp.float32, 0.0, 0.999973)
        return (x, src, dst, edge_attr_20, edge_attr_3, edge_attr_8, edge_attr_8_n2, edge_weight)
    x, src, dst, edge_attr_20, edge_attr_3, edge_attr_8, edge_attr_8_n2, edge_weight = _rec_inputs()

    def _L0_gnn_setup():
        import jax, jax.numpy as jnp
        import numpy as np
        N = 625
        E = 20000
        D = 512
        H = 8
        DH = D // H
        EPS = 1e-05

        def layer_norm(x, g, b):
            mu = x.mean(-1, keepdims=True)
            var = ((x - mu) ** 2).mean(-1, keepdims=True)
            return (x - mu) * jax.lax.rsqrt(var + EPS) * g + b
        key = jax.random.key(seed)
        ks = jax.random.split(key, 12)
        return dict(node_feature=jax.random.normal(ks[0], (N, D), jnp.float32), src=jax.random.randint(ks[1], (E,), 0, N, dtype=jnp.int32), dst=jax.random.randint(ks[2], (E,), 0, N, dtype=jnp.int32), dist_attn=jax.random.normal(ks[3], (E, H), jnp.float32), path_attn=jax.random.normal(ks[4], (E, H), jnp.float32), Wqkv=jax.random.normal(ks[5], (D, 3 * D), jnp.float32) / np.float32(np.sqrt(D)), bqkv=jnp.zeros((3 * D,), jnp.float32), Wo=jax.random.normal(ks[6], (D, D), jnp.float32) / np.float32(np.sqrt(D)), bo=jnp.zeros((D,), jnp.float32), ln1_g=jnp.ones((D,), jnp.float32), ln1_b=jnp.zeros((D,), jnp.float32), W1=jax.random.normal(ks[7], (D, 4 * D), jnp.float32) / np.float32(np.sqrt(D)), b1=jnp.zeros((4 * D,), jnp.float32), W2=jax.random.normal(ks[8], (4 * D, D), jnp.float32) / np.float32(np.sqrt(4 * D)), b2=jnp.zeros((D,), jnp.float32), ln2_g=jnp.ones((D,), jnp.float32), ln2_b=jnp.zeros((D,), jnp.float32))
    _L0_gnn_all = _L0_gnn_setup()
    _L0_gnn_in = {k: v for k, v in _L0_gnn_all.items() if k in ('Wqkv', 'bqkv', 'Wo', 'bo', 'ln1_g', 'ln1_b', 'W1', 'b1', 'W2', 'b2', 'ln2_g', 'ln2_b')}
    del _L0_gnn_all

    def _L1_gnn_setup():
        import jax, jax.numpy as jnp
        import numpy as np
        N_ATOMS = 5000
        N_EDGES = 50000
        C = 128
        F = 128
        N_RBF = 20
        LOG2 = float(np.log(2.0))
        Y0 = float(1.0 / np.sqrt(4.0 * np.pi))
        Y1_SCALE = float(np.sqrt(3.0 / (4.0 * np.pi)))

        def shifted_softplus(x):
            return jax.nn.softplus(x) - LOG2

        def _forward(x, idx_i, idx_j, f_ij, rcut_ij, r_ij, W_in2f_s, W_in2f_v, Wf1, bf1, Wf2, bf2, W1_s, W1_v, W2_s, W2_v):
            n = x.shape[0]
            e = r_ij.shape[0]
            xs = x[:, :C] @ (W_in2f_s / np.sqrt(C))
            xv = jnp.einsum('nci,cf->nfi', x[:, C:].reshape(n, C, 3), W_in2f_v) / np.sqrt(C)
            sj = xs[idx_j]
            vj = xv[idx_j]
            u = r_ij / jnp.linalg.norm(r_ij, axis=-1, keepdims=True)
            Yv = Y1_SCALE * u
            o0a = sj * Y0
            o0b = jnp.einsum('efi,ei->ef', vj, Yv) / np.sqrt(3.0)
            s2 = jnp.stack([o0a, o0b], axis=-1).reshape(e, 2 * F)
            ova = sj[:, :, None] * Yv[:, None, :]
            ovb = vj * Y0
            v2 = jnp.stack([ova, ovb], axis=2)
            w1 = jnp.cross(vj, Yv[:, None, :]) / np.sqrt(2.0)
            ax, ay, az = (vj[..., 0], vj[..., 1], vj[..., 2])
            bx, by, bz = (Yv[:, None, 0], Yv[:, None, 1], Yv[:, None, 2])
            t = jnp.stack([(ax * by + ay * bx) / np.sqrt(2.0), (ay * bz + az * by) / np.sqrt(2.0), (2.0 * az * bz - ax * bx - ay * by) / np.sqrt(6.0), (az * bx + ax * bz) / np.sqrt(2.0), (ax * bx - ay * by) / np.sqrt(2.0)], axis=-1)
            h = shifted_softplus(f_ij @ Wf1 + bf1)
            W = (h @ Wf2 + bf2) * rcut_ij[:, None]
            m_s = s2 * W[:, :2 * F]
            m_v = (v2.reshape(e, 2 * F, 3) * W[:, 2 * F:4 * F, None]).reshape(e, 6 * F)
            m_w = (w1 * W[:, 4 * F:5 * F, None]).reshape(e, 3 * F)
            m_t = (t * W[:, 5 * F:6 * F, None]).reshape(e, 5 * F)
            x_ij = jnp.concatenate([m_s, m_v, m_w, m_t], axis=1)
            agg = jax.ops.segment_sum(x_ij, idx_i, num_segments=n)
            S = agg[:, :2 * F] @ (W1_s / np.sqrt(2 * F))
            V = jnp.einsum('nmi,mc->nci', agg[:, 2 * F:8 * F].reshape(n, 2 * F, 3), W1_v) / np.sqrt(2 * F)
            S = shifted_softplus(S)
            S = S @ (W2_s / np.sqrt(C))
            V = jnp.einsum('nci,cd->ndi', V, W2_v) / np.sqrt(C)
            return jnp.concatenate([S, V.reshape(n, 3 * C)], axis=1)
        key = jax.random.key(seed)
        ks = jax.random.split(key, 16)
        f32 = jnp.float32
        x = jax.random.normal(ks[0], (N_ATOMS, 4 * C), f32)
        idx_i = jnp.sort(jax.random.randint(ks[1], (N_EDGES,), 0, N_ATOMS))
        idx_j = jax.random.randint(ks[2], (N_EDGES,), 0, N_ATOMS)
        f_ij = jax.random.uniform(ks[3], (N_EDGES, N_RBF), f32)
        rcut_ij = jax.random.uniform(ks[4], (N_EDGES,), f32)
        r_ij = jax.random.normal(ks[5], (N_EDGES, 3), f32)
        W_in2f_s = jax.random.normal(ks[6], (C, F), f32)
        W_in2f_v = jax.random.normal(ks[7], (C, F), f32)
        Wf1 = jax.random.normal(ks[8], (N_RBF, F), f32) / np.sqrt(N_RBF)
        bf1 = 0.1 * jax.random.normal(ks[9], (F,), f32)
        Wf2 = jax.random.normal(ks[10], (F, 6 * F), f32) / np.sqrt(F)
        bf2 = 0.1 * jax.random.normal(ks[11], (6 * F,), f32)
        W1_s = jax.random.normal(ks[12], (2 * F, C), f32)
        W1_v = jax.random.normal(ks[13], (2 * F, C), f32)
        W2_s = jax.random.normal(ks[14], (C, C), f32)
        W2_v = jax.random.normal(ks[15], (C, C), f32)
        return dict(x=x, idx_i=idx_i, idx_j=idx_j, f_ij=f_ij, rcut_ij=rcut_ij, r_ij=r_ij, W_in2f_s=W_in2f_s, W_in2f_v=W_in2f_v, Wf1=Wf1, bf1=bf1, Wf2=Wf2, bf2=bf2, W1_s=W1_s, W1_v=W1_v, W2_s=W2_s, W2_v=W2_v)
    _L1_gnn_all = _L1_gnn_setup()
    _L1_gnn_in = {k: v for k, v in _L1_gnn_all.items() if k in ('W_in2f_s', 'W_in2f_v', 'Wf1', 'bf1', 'Wf2', 'bf2', 'W1_s', 'W1_v', 'W2_s', 'W2_v')}
    del _L1_gnn_all
    return {'x': x, 'src': src, 'dst': dst, 'edge_attr_20': edge_attr_20, 'edge_attr_3': edge_attr_3, 'edge_attr_8': edge_attr_8, 'edge_attr_8_n2': edge_attr_8_n2, 'edge_weight': edge_weight, 'L0_gnn_Wqkv': _L0_gnn_in['Wqkv'], 'L0_gnn_bqkv': _L0_gnn_in['bqkv'], 'L0_gnn_Wo': _L0_gnn_in['Wo'], 'L0_gnn_bo': _L0_gnn_in['bo'], 'L0_gnn_ln1_g': _L0_gnn_in['ln1_g'], 'L0_gnn_ln1_b': _L0_gnn_in['ln1_b'], 'L0_gnn_W1': _L0_gnn_in['W1'], 'L0_gnn_b1': _L0_gnn_in['b1'], 'L0_gnn_W2': _L0_gnn_in['W2'], 'L0_gnn_b2': _L0_gnn_in['b2'], 'L0_gnn_ln2_g': _L0_gnn_in['ln2_g'], 'L0_gnn_ln2_b': _L0_gnn_in['ln2_b'], 'L1_gnn_W_in2f_s': _L1_gnn_in['W_in2f_s'], 'L1_gnn_W_in2f_v': _L1_gnn_in['W_in2f_v'], 'L1_gnn_Wf1': _L1_gnn_in['Wf1'], 'L1_gnn_bf1': _L1_gnn_in['bf1'], 'L1_gnn_Wf2': _L1_gnn_in['Wf2'], 'L1_gnn_bf2': _L1_gnn_in['bf2'], 'L1_gnn_W1_s': _L1_gnn_in['W1_s'], 'L1_gnn_W1_v': _L1_gnn_in['W1_v'], 'L1_gnn_W2_s': _L1_gnn_in['W2_s'], 'L1_gnn_W2_v': _L1_gnn_in['W2_v']}

def reference(x, src, dst, edge_attr_20, edge_attr_3, edge_attr_8, edge_attr_8_n2, edge_weight, L0_gnn_Wqkv, L0_gnn_bqkv, L0_gnn_Wo, L0_gnn_bo, L0_gnn_ln1_g, L0_gnn_ln1_b, L0_gnn_W1, L0_gnn_b1, L0_gnn_W2, L0_gnn_b2, L0_gnn_ln2_g, L0_gnn_ln2_b, L1_gnn_W_in2f_s, L1_gnn_W_in2f_v, L1_gnn_Wf1, L1_gnn_bf1, L1_gnn_Wf2, L1_gnn_bf2, L1_gnn_W1_s, L1_gnn_W1_v, L1_gnn_W2_s, L1_gnn_W2_v):
    import jax
    import jax.numpy as jnp

    def _L0_gnn_ref(node_feature, src, dst, dist_attn, path_attn, Wqkv, bqkv, Wo, bo, ln1_g, ln1_b, W1, b1, W2, b2, ln2_g, ln2_b):
        import jax, jax.numpy as jnp
        import numpy as np
        N = 625
        E = 20000
        D = 512
        H = 8
        DH = D // H
        EPS = 1e-05

        def layer_norm(x, g, b):
            mu = x.mean(-1, keepdims=True)
            var = ((x - mu) ** 2).mean(-1, keepdims=True)
            return (x - mu) * jax.lax.rsqrt(var + EPS) * g + b
        h = layer_norm(node_feature, ln1_g, ln1_b)
        qkv = (h @ Wqkv + bqkv).reshape(N, 3, H, DH)
        q = qkv[:, 0] * D ** (-0.5)
        k = qkv[:, 1]
        v = qkv[:, 2]
        logits = jnp.einsum('ehd,ehd->eh', q[src], k[dst])
        a = logits + dist_attn + path_attn
        mx = jax.ops.segment_max(a, dst, num_segments=N)
        e = jnp.exp(a - mx[dst])
        s = jax.ops.segment_sum(e, dst, num_segments=N)
        sa = e / s[dst]
        msg = v[src] * sa[:, :, None]
        agg = jax.ops.segment_sum(msg, dst, num_segments=N).reshape(N, D)
        x = agg @ Wo + bo
        h1 = node_feature + x
        h2 = layer_norm(h1, ln2_g, ln2_b)
        h2 = jax.nn.gelu(h2 @ W1 + b1, approximate=False) @ W2 + b2
        return h1 + h2

    def _L1_gnn_ref(x, idx_i, idx_j, f_ij, rcut_ij, r_ij, W_in2f_s, W_in2f_v, Wf1, bf1, Wf2, bf2, W1_s, W1_v, W2_s, W2_v):
        import jax, jax.numpy as jnp
        import numpy as np
        N_ATOMS = 5000
        N_EDGES = 50000
        C = 128
        F = 128
        N_RBF = 20
        LOG2 = float(np.log(2.0))
        Y0 = float(1.0 / np.sqrt(4.0 * np.pi))
        Y1_SCALE = float(np.sqrt(3.0 / (4.0 * np.pi)))

        def shifted_softplus(x):
            return jax.nn.softplus(x) - LOG2

        def _forward(x, idx_i, idx_j, f_ij, rcut_ij, r_ij, W_in2f_s, W_in2f_v, Wf1, bf1, Wf2, bf2, W1_s, W1_v, W2_s, W2_v):
            n = x.shape[0]
            e = r_ij.shape[0]
            xs = x[:, :C] @ (W_in2f_s / np.sqrt(C))
            xv = jnp.einsum('nci,cf->nfi', x[:, C:].reshape(n, C, 3), W_in2f_v) / np.sqrt(C)
            sj = xs[idx_j]
            vj = xv[idx_j]
            u = r_ij / jnp.linalg.norm(r_ij, axis=-1, keepdims=True)
            Yv = Y1_SCALE * u
            o0a = sj * Y0
            o0b = jnp.einsum('efi,ei->ef', vj, Yv) / np.sqrt(3.0)
            s2 = jnp.stack([o0a, o0b], axis=-1).reshape(e, 2 * F)
            ova = sj[:, :, None] * Yv[:, None, :]
            ovb = vj * Y0
            v2 = jnp.stack([ova, ovb], axis=2)
            w1 = jnp.cross(vj, Yv[:, None, :]) / np.sqrt(2.0)
            ax, ay, az = (vj[..., 0], vj[..., 1], vj[..., 2])
            bx, by, bz = (Yv[:, None, 0], Yv[:, None, 1], Yv[:, None, 2])
            t = jnp.stack([(ax * by + ay * bx) / np.sqrt(2.0), (ay * bz + az * by) / np.sqrt(2.0), (2.0 * az * bz - ax * bx - ay * by) / np.sqrt(6.0), (az * bx + ax * bz) / np.sqrt(2.0), (ax * bx - ay * by) / np.sqrt(2.0)], axis=-1)
            h = shifted_softplus(f_ij @ Wf1 + bf1)
            W = (h @ Wf2 + bf2) * rcut_ij[:, None]
            m_s = s2 * W[:, :2 * F]
            m_v = (v2.reshape(e, 2 * F, 3) * W[:, 2 * F:4 * F, None]).reshape(e, 6 * F)
            m_w = (w1 * W[:, 4 * F:5 * F, None]).reshape(e, 3 * F)
            m_t = (t * W[:, 5 * F:6 * F, None]).reshape(e, 5 * F)
            x_ij = jnp.concatenate([m_s, m_v, m_w, m_t], axis=1)
            agg = jax.ops.segment_sum(x_ij, idx_i, num_segments=n)
            S = agg[:, :2 * F] @ (W1_s / np.sqrt(2 * F))
            V = jnp.einsum('nmi,mc->nci', agg[:, 2 * F:8 * F].reshape(n, 2 * F, 3), W1_v) / np.sqrt(2 * F)
            S = shifted_softplus(S)
            S = S @ (W2_s / np.sqrt(C))
            V = jnp.einsum('nci,cd->ndi', V, W2_v) / np.sqrt(C)
            return jnp.concatenate([S, V.reshape(n, 3 * C)], axis=1)
        return _forward(x, idx_i, idx_j, f_ij, rcut_ij, r_ij, W_in2f_s, W_in2f_v, Wf1, bf1, Wf2, bf2, W1_s, W1_v, W2_s, W2_v)
    h = jnp.maximum(_layernorm(x, axis=-1), 0.0)
    x = x + _L0_gnn_ref(h, src, dst, edge_attr_8, edge_attr_8_n2, L0_gnn_Wqkv, L0_gnn_bqkv, L0_gnn_Wo, L0_gnn_bo, L0_gnn_ln1_g, L0_gnn_ln1_b, L0_gnn_W1, L0_gnn_b1, L0_gnn_W2, L0_gnn_b2, L0_gnn_ln2_g, L0_gnn_ln2_b)
    h = jnp.maximum(_layernorm(x, axis=-1), 0.0)
    x = x + _L1_gnn_ref(h, src, dst, edge_attr_20, edge_weight, edge_attr_3, L1_gnn_W_in2f_s, L1_gnn_W_in2f_v, L1_gnn_Wf1, L1_gnn_bf1, L1_gnn_Wf2, L1_gnn_bf2, L1_gnn_W1_s, L1_gnn_W1_v, L1_gnn_W2_s, L1_gnn_W2_v)
    return x

_drawn_inputs = setup_inputs


def setup_inputs(seed=0):
    import zlib

    import numpy as np

    out = dict(_drawn_inputs(seed))
    spreads = {'L0_gnn_bqkv': (0.0, 0.1),
     'L0_gnn_bo': (0.0, 0.1),
     'L0_gnn_ln1_g': (1.0, 0.2),
     'L0_gnn_ln1_b': (0.0, 0.1),
     'L0_gnn_b1': (0.0, 0.1),
     'L0_gnn_b2': (0.0, 0.1),
     'L0_gnn_ln2_g': (1.0, 0.2),
     'L0_gnn_ln2_b': (0.0, 0.1)}
    factors = {'L1_gnn_bf1': 2.716}
    for name, (base, spread) in spreads.items():
        noise = np.random.default_rng([zlib.crc32(name.encode()), seed]).standard_normal(out[name].shape)
        drawn = base * np.exp(spread * noise) if base else spread * noise
        out[name] = jnp.asarray(drawn.astype(out[name].dtype))
    for name, factor in factors.items():
        out[name] = (out[name] * factor).astype(out[name].dtype)
    return out
```

```python
import concourse.bass as bass
from concourse import mybir
from contextlib import ExitStack


def gnn_two_layer_kernel(nc: bass.Bass, A: dict, out: bass.AP, debug=False):
    F32 = mybir.dt.float32
    I32 = mybir.dt.int32
    BF16 = mybir.dt.bfloat16
    ALU = mybir.AluOpType
    ACT = mybir.ActivationFunctionType
    X_AXIS = mybir.AxisListType.X
    ds = bass.ds

    P = 128
    N, D = A["x"].shape
    E = A["src"].shape[0]
    H = A["edge_attr_8"].shape[1]
    DH = D // H
    NRBF = A["edge_attr_20"].shape[1]
    C = A["L1_gnn_W_in2f_s"].shape[0]
    FD = A["L0_gnn_W1"].shape[1]
    KT = D // P
    FT = FD // P
    NT = -(-N // P)
    NP = NT * P
    NH = NP // 2
    ROWS = [min(P, N - P * t) for t in range(NT)]
    EP = next(p for p in range(P, 0, -1) if E % p == 0)
    EC = E // EP
    CH = (E + NT * (P - 1)) // P
    CH += -CH % 4
    SLOTS = CH * P
    W0 = 2 + H
    W1 = 6 + NRBF
    HF = C // 2
    G4 = 4
    QB = 21
    QUADS = CH // 4
    BIG = 1e30
    EPS = 1e-5
    LOG2 = 0.6931471805599453
    Y0 = (4.0 * 3.141592653589793) ** -0.5
    Y1 = (3.0 / (4.0 * 3.141592653589793)) ** 0.5
    RC = C ** -0.5
    R2F = (2 * C) ** -0.5
    NCOMP = 8
    COMP_SCALE = [Y0 * RC * R2F, Y1 * RC * R2F * 3 ** -0.5] + [Y0 * RC * R2F] * 3 + [Y1 * RC * R2F] * 3
    assert CH % QB == 0 and CH % G4 == 0 and QB * 3 * H <= 512 and D == 4 * C

    ctx = ExitStack()
    with ctx:
        def sb(name, shape, dt=F32):
            return ctx.enter_context(nc.sbuf_tensor(name, shape, dt))

        def dram(name, shape, dt=F32):
            return nc.dram_tensor(name, shape, dt, kind="ExternalOutput" if debug else "Internal")

        q_table = dram("q_table", [N, D])
        v_table = dram("v_table", [N, D])
        slots_dram = [dram("slots0_dram", [SLOTS, W0]), dram("slots1_dram", [SLOTS, W1])]
        x_table = [dram(f"x_table{h}", [N, 4 * HF]) for h in range(2)]

        def region(tensor):
            at = [0]

            def carve(width, dt=F32, parts=P):
                words = width if dt != BF16 else width // 2
                a = tensor[0:parts, at[0]:at[0] + words]
                at[0] += words
                assert at[0] <= tensor.shape[1], (at[0], tensor.shape)
                return a if dt == F32 else a.bitcast(dt)
            return carve

        X = sb("X", [P, NT, D])
        H0 = sb("H0", [P, NT * D])
        HN = sb("HN", [P, NT * D])
        HT = sb("HT", [P, KT * NP])
        BIG1 = sb("BIG1", [P, 2 * FT * D])
        ARENA = sb("ARENA", [P, FT * NP])
        WO = sb("WO", [P, KT, D])
        h0 = H0[:, :].rearrange("p (t n) -> p t n", t=NT)
        hn = HN[:, :].rearrange("p (t n) -> p t n", t=NT)
        ht = HT[:, :].rearrange("p (k n) -> p k n", k=KT)
        wqkv = BIG1[:, 0:KT * 3 * D].rearrange("p (k n) -> p k n", k=KT)
        w1 = BIG1[:, 0:KT * FD].rearrange("p (k n) -> p k n", k=KT)
        w2 = BIG1[:, FT * D:].rearrange("p (f n) -> p f n", f=FT)
        gelu_t = ARENA[:, :].rearrange("p (f n) -> p f n", f=FT)

        carve = region(BIG1[:, FT * D:])
        raw0 = carve(2 * EC * H, parts=EP).rearrange("p (a c h) -> p a c h", a=2, h=H)
        raw_r = carve(EC * 3, parts=EP).rearrange("p (c i) -> p c i", i=3)
        rsq = carve(EC * 3, parts=EP).rearrange("p (c i) -> p c i", i=3)
        rnorm = carve(EC * 2, parts=EP).rearrange("p (a c) -> p a c", a=2)
        pack = [carve(EC * w, parts=EP).rearrange("p (c w) -> p c w", w=w) for w in (W0, W1)]
        keyf = carve(2 * EC, parts=EP).rearrange("p (k c) -> p k c", k=2)
        ge = carve((NT + 1) * EC, parts=EP).rearrange("p (t c) -> p t c", c=EC)
        in_b = carve(NT * EC, parts=EP).rearrange("p (t c) -> p t c", c=EC)
        cum = carve(NT * EC, parts=EP).rearrange("p (t c) -> p t c", c=EC)
        carve = region(BIG1[:, FT * D:])
        OTb = carve(SLOTS, BF16)
        carve = region(ARENA)
        K_sb = carve(NT * D).rearrange("p (t n) -> p t n", t=NT)
        qg = carve(2 * D).rearrange("p (u n) -> p u n", u=2)
        msg = carve(2 * D).rearrange("p (u n) -> p u n", u=2)
        masked = carve(2 * H * P).rearrange("p (u h n) -> p u h n", u=2, h=H)
        qst = carve(2 * 2 * D).rearrange("p (u a n) -> p u a n", u=2, a=2)
        h_t = BIG1[:, 0:SLOTS]
        carve = region(BIG1[:, SLOTS:])
        agg_t = carve(NCOMP * NP).rearrange("p (m n) -> p m n", m=NCOMP)
        carve = region(ARENA)
        agg1 = carve(NT * NCOMP * C).rearrange("p (t m f) -> p t m f", t=NT, m=NCOMP)
        s_z = carve(NP)
        s_e = carve(NP)
        s_t = carve(NP)
        v_t = carve(3 * NP).rearrange("p (i n) -> p i n", i=3)
        carve = region(HN)
        M = carve(2 * 2 * 9 * HF).rearrange("p (w u m f) -> p w u m f", w=2, u=2, m=9)
        carve = region(H0)
        xg = carve(2 * 2 * 4 * HF).rearrange("p (w u j f) -> p w u j f", w=2, u=2, j=4)
        hs = carve(2 * 2 * P).rearrange("p (w n) -> p w n", w=2)
        xvu = carve(2 * 3 * HF).rearrange("p (u i f) -> p u i f", u=2, i=3)
        dotu = carve(2 * HF).rearrange("p (u f) -> p u f", u=2)
        carve = region(HT)
        xst = carve(2 * D).rearrange("p (r h j f) -> p r h j f", r=2, h=2, j=4)
        carve = region(HN)
        fs = carve(2 * G4 * NRBF).rearrange("p (w n) -> p w n", w=2)
        ft = carve(2 * 512).rearrange("p (w n) -> p w n", w=2)
        carve = region(ARENA)
        zed = carve(2 * 512).rearrange("p (w n) -> p w n", w=2)
        zab = carve(2 * 512).rearrange("p (w n) -> p w n", w=2)
        zln = carve(2 * 512).rearrange("p (w n) -> p w n", w=2)

        keyi = sb("keyi", [EP, 2, EC], I32)
        zer = sb("zer", [P, CH])
        small = sb("small", [P, 2, 4, NT])
        small_i = sb("small_i", [P, 2, NT], I32)
        start = sb("start", [P, 2, NT])
        offs = sb("offs", [P, 2, NT])
        pos = sb("pos", [EP, 2, EC], I32)
        iota_c = sb("iota_c", [P, CH])
        iota_n = sb("iota_n", [P, P])
        tilef = sb("tilef", [P, 2, CH])
        tilei = sb("tilei", [P, 2, CH], I32)
        slots0 = sb("slots0", [P, CH, W0])
        slots1 = sb("slots1", [P, CH, W1])
        slots = [slots0, slots1]
        row_st = sb("row_st", [EP, 2, W1])
        pos_st = sb("pos_st", [EP, 2, 1], I32)
        idx_st = sb("idx_st", [P, 4, 1], I32)
        local = sb("local", [P, 2, CH])
        gidx = sb("gidx", [P, 2, CH], I32)
        logit = sb("logit", [P, CH, H])
        araw = sb("araw", [P, 2, H])
        cmax = sb("cmax", [P, CH, H])
        eqt = sb("eqt", [P, NT, CH])
        nmax = sb("nmax", [P, NT, H])
        mc = sb("mc", [P, CH, H])
        mc3 = sb("mc3", [P, CH, 3, H], BF16)
        O = sb("O", [P, 4, P])
        pen = sb("pen", [P, 2, P])
        OTf = sb("OTf", [P, 2, P])
        ident = sb("ident", [P, P])
        ones = sb("ones", [P, P])
        tri = sb("tri", [P, P])
        stats = sb("stats", [P, NT, 6])
        mv = sb("mv", [P, NT, 2])
        std = sb("std", [P, NT])
        rstd = sb("rstd", [P, NT])
        eps = sb("eps", [P, 1])
        lnp = sb("lnp", [P, 4, KT])
        b1col = sb("b1col", [P, FT])
        brow = sb("brow", [P, 3 * D])
        den = sb("den", [P, 2, NT * H])
        wf1 = sb("wf1", [NRBF, C])
        bf1 = sb("bf1", [C, 1])
        wf2 = sb("wf2", [P, 2, 4 * HF])
        bf2 = sb("bf2", [1, 2, 4 * HF])
        wfr = mc[:, :, :].rearrange("p c h -> p (c h)")[:, 0:4 * C]
        zero_w = sb("zero_w", [P, 512])
        win = sb("win", [P, 2, C])
        w1sv = sb("w1sv", [P, 2, 2, C])
        w2sv = sb("w2sv", [P, 2, C])
        bfraw = cmax[0:1, :, :].rearrange("p c h -> p (c h)")[:, 0:4 * C]

        PS = ctx.enter_context(nc.psum_tensor("PS", [P, 8, 512], F32))

        def pair(b):
            return PS[:, b:b + 2, :].rearrange("p b n -> p (b n)")

        def XB(t):
            return (4, 5, 6, 7, 2)[t]

        def OB(t):
            return (2, 3, 4, 5, 6)[t]

        sems = {}

        def S(name):
            if name not in sems:
                sems[name] = ctx.enter_context(nc.semaphore(name))
            return sems[name]

        class Chain:

            def __init__(self, eng, name):
                self.eng, self.sem, self.n = eng, S(name), 0

            def __call__(self, ins):
                self.n += 1
                ins.then_inc(self.sem, 1)
                self.eng.wait_ge(self.sem, self.n)

        class LoopChain:

            def __init__(self, eng, name, per):
                self.eng, self.sem, self.per, self.n, self.base = eng, S(name), per, 0, 0

            def turn(self, i):
                assert self.n in (0, self.per), self.n
                self.i, self.n = i, 0

            def __call__(self, ins):
                self.n += 1
                ins.then_inc(self.sem, 1)
                self.eng.wait_ge(self.sem, self.base + self.i * self.per + self.n)

            def mark(self, ins):
                self.n += 1
                ins.then_inc(self.sem, 1)
                return self.base + self.i * self.per + self.n

        block = ctx.enter_context(nc.Block())

        @block.sync
        def _(sp):
            sp.dma_start(keyi[:, 0, :], A["dst"].rearrange("(p c) -> p c", p=EP)).then_inc(S("ld_keys"), 16)
            sp.dma_start(keyi[:, 1, :], A["src"].rearrange("(p c) -> p c", p=EP)).then_inc(S("ld_keys"), 16)
            for t in range(NT):
                if ROWS[t] == P:
                    continue
                sp.wait_ge(S("x_pad"), 1)
            for t in range(NT):
                sp.dma_start(X[0:ROWS[t], t, :], A["x"][P * t:P * t + ROWS[t], :]).then_inc(S("ld_x"), 16)
            for a, name in enumerate(("edge_attr_8", "edge_attr_8_n2")):
                sp.dma_start(raw0[:, a, :, :],
                             A[name].rearrange("(p c) h -> p c h", p=EP)).then_inc(S("ld_bias"), 16)
            sp.dma_start(raw_r, A["edge_attr_3"].rearrange("(p c) i -> p c i", p=EP)).then_inc(S("ld_r"), 16)
            sp.dma_start(rnorm[:, 1, :], A["edge_weight"].rearrange("(p c) -> p c", p=EP)).then_inc(S("ld_r"), 16)
            sp.dma_start(pack[1][:, :, 6:W1], A["edge_attr_20"].rearrange("(p c) f -> p c f", p=EP)).then_inc(S("ld_f"), 16)
            sp.dma_start(wqkv, A["L0_gnn_Wqkv"].rearrange("(k p) n -> p k n", p=P)).then_inc(S("ld_wqkv"), 16)
            sp.dma_start(brow[:, :], A["L0_gnn_bqkv"].rearrange("(a n) -> a n", a=1).to_broadcast([P, 3 * D])).then_inc(S("ld_brow"), 16)
            for k in range(2):
                sp.wait_ge(S("dummy"), k + 1)
                w = (W0, W1)[k]
                sp.dma_start(slots_dram[k][:, :].rearrange("(p c) w -> p c w", p=P),
                             slots[k][:, :, :]).then_inc(S(f"filled{k}"), 16)
            for t in range(NT):
                sp.wait_ge(S("qv_rows"), t + 1)
                r = ROWS[t]
                sp.dma_start(q_table[P * t:P * t + r, :], qst[0:r, t % 2, 0, :]).then_inc(S(f"st_qv{t % 2}"), 16)
                sp.dma_start(v_table[P * t:P * t + r, :], qst[0:r, t % 2, 1, :]).then_inc(S(f"st_qv{t % 2}"), 16)
            for k in range(2):
                sp.wait_ge(S(f"scattered{k}a"), 16 * (EC // 2))
                sp.wait_ge(S(f"scattered{k}b"), 16 * (EC // 2))
                sp.dma_start(slots[k][:, :, :],
                             slots_dram[k][:, :].rearrange("(c p) w -> p c w", p=P)).then_inc(S(f"ld_slots{k}"), 16)
            sp.wait_ge(S("qkv_mm"), 3 * NT)
            sp.dma_start(w1, A["L0_gnn_W1"].rearrange("(k p) n -> p k n", p=P)).then_inc(S("ld_w1"), 16)
            sp.wait_ge(S("qkv_sb"), 3 * NT)
            for j, name in enumerate(("L0_gnn_bo", "L0_gnn_b2")):
                sp.dma_start(brow[:, j * D:(j + 1) * D], A[name].rearrange("(a n) -> a n", a=1).to_broadcast([P, D])
                             ).then_inc(S("ld_b2rows"), 16)
            sp.wait_ge(S("shifted"), 1)
            sp.dma_start(wfr, A["L1_gnn_Wf2"][:, 0:4 * C]).then_inc(S("ld_wf2"), 16)
            sp.dma_start(bfraw, A["L1_gnn_bf2"][0:4 * C].rearrange("(a n) -> a n", a=1)).then_inc(S("ld_wf2"), 16)
            sp.wait_ge(S("mx_mm"), CH)
            sp.dma_start(w2, A["L0_gnn_W2"].rearrange("(f p) n -> p f n", p=P)).then_inc(S("ld_w2"), 16)
            for t in range(NT):
                sp.wait_ge(S("x_rows"), t + 1)
                r = ROWS[t]
                for h in range(2):
                    sp.dma_start(x_table[h][P * t:P * t + r, :],
                                 xst[0:r, t % 2, h, :, :].rearrange("p j f -> p (j f)")).then_inc(S(f"st_x{t % 2}"), 16)
            for t in range(NT):
                sp.wait_ge(S("out_rows"), t + 1)
                sp.dma_start(out[P * t:P * t + ROWS[t], :], X[0:ROWS[t], t, :]).then_inc(S("st_out"), 16)
            sp.wait_ge(S("st_out"), 16 * NT)

        @block.gpsimd
        def _(pool):
            link = Chain(pool, "pool_chain")
            pool.memset(X[:, NT - 1, :], 0.0).then_inc(S("x_pad"), 1)
            pool.memset(zer[:, :], 0.0).then_inc(S("consts"), 1)
            pool.memset(zero_w[:, :], 0.0)
            pool.memset(eps[:, :], EPS).then_inc(S("consts"), 1)
            pool.memset(ones[:, :], 1.0).then_inc(S("consts"), 1)
            link(pool.memset(ident[:, :], 0.0))
            pool.affine_select(out=ident[:, :], in_=ident[:, :], compare_op=ALU.not_equal, fill=1.0, base=0,
                               pattern=[[-1, P]], channel_multiplier=1).then_inc(S("consts"), 1)
            link(pool.memset(tri[:, :], 1.0))
            pool.affine_select(out=tri[:, :], in_=tri[:, :], compare_op=ALU.is_gt, fill=0.0, base=0,
                               pattern=[[1, P]], channel_multiplier=-1).then_inc(S("consts"), 1)
            pool.iota(iota_n[:, :], pattern=[[1, P]], base=0, channel_multiplier=0,
                      allow_small_or_imprecise_dtypes=True).then_inc(S("consts"), 1)
            pool.iota(iota_c[:, :], pattern=[[1, CH]], base=0, channel_multiplier=0,
                      allow_small_or_imprecise_dtypes=True).then_inc(S("consts"), 1)
            link(pool.memset(slots0[:, :, :], 0.0))
            pool.memset(slots0[:, :, 0:1], -1.0).then_inc(S("dummy"), 1)
            link(pool.memset(slots1[:, :, :], 0.0))
            pool.memset(slots1[:, :, 0:1], -1.0).then_inc(S("dummy"), 1)

            for k, w in enumerate((W0, W1)):
                pool.wait_ge(S("packed"), k + 1)
                pool.wait_ge(S(f"filled{k}"), 16)
                if k:
                    for half in "ab":
                        pool.wait_ge(S(f"scattered0{half}"), 16 * (EC // 2))
                def stage_and_scatter(i, u, half):
                        pool.tensor_copy(out=row_st[:, u, 0:w],
                                         in_=pack[k][:, ds(i * 2 + u, 1), :].rearrange("p a w -> p (a w)")
                                         ).then_inc(S(f"staged{k}"), 1)
                        pool.tensor_copy(out=pos_st[:, u, :], in_=pos[:, k, ds(i * 2 + u, 1)]).then_inc(S(f"staged{k}"), 1)
                        pool.wait_ge(S(f"staged{k}"), i * 4 + 2 * u + 2)
                        pool.sem_inc(S(f"scatter_go{k}"), 1)
                        pool.indirect_dma_start(
                            out=slots_dram[k][:, :], out_offset=bass.IndirectOffsetOnAxis(ap=pos_st[:, u, :], axis=0),
                            in_=row_st[:, u, 0:w], in_offset=None).then_inc(S(f"scattered{k}{half}"), 16)

                stage_and_scatter(0, 0, "a")
                stage_and_scatter(0, 1, "b")
                with pool.Fori(1, EC // 2) as i:
                    for u, half in enumerate("ab"):
                        pool.wait_ge(S(f"scattered{k}{half}"), i * 16)
                        stage_and_scatter(i, u, half)

            def gather_q(c, u, last_use):
                pool.wait_ge(S("prod_done"), c + 1)
                pool.tensor_copy(out=idx_st[:, u, :], in_=gidx[:, 0, ds(c, 1)]).then_inc(S("idx0"), 1)
                pool.wait_ge(S("idx0"), c + 1)
                pool.sem_inc(S("gather_go"), 1)
                pool.indirect_dma_start(out=qg[:, u, :], out_offset=None, in_=q_table[:, :],
                                        in_offset=bass.IndirectOffsetOnAxis(ap=idx_st[:, u, :], axis=0)
                                        ).then_inc(S(f"q_in{u}"), 16)

            def mask(c, u):
                pool.wait_ge(S("logit_done"), c + 1)
                pool.wait_ge(S("mask_t"), c + 1)
                pool.tensor_tensor(
                    out=masked[:, u, :, :],
                    in0=pen[:, u, :].unsqueeze(1).to_broadcast([P, H, P]),
                    in1=logit[:, ds(c, 1), :].rearrange("p a h -> p (a h)").unsqueeze(2).to_broadcast([P, H, P]),
                    op=ALU.add).then_inc(S("mask_done"), 1)

            pool.wait_ge(S("slots_ready"), 1)
            for u in range(2):
                pool.wait_ge(S(f"st_qv{u}"), 32 * len(range(u, NT, 2)))
            gather_q(0, 0, 0)
            with pool.Fori(0, CH // 2 - 1) as i:
                gather_q(i * 2 + 1, 1, 0)
                mask(i * 2, 0)
                gather_q(i * 2 + 2, 0, 0)
                mask(i * 2 + 1, 1)
            gather_q(CH - 1, 1, 0)
            mask(CH - 2, 0)
            mask(CH - 1, 1)

            pool.wait_ge(S("prod_done"), CH + 2)
            with pool.Fori(0, CH // 2) as i:
                for u in range(2):
                    pool.wait_ge(S("msg_done"), i * 2 + u + 1)
                    pool.tensor_copy(out=idx_st[:, u, :], in_=gidx[:, 0, ds(i * 2 + u, 1)]).then_inc(S("idx1"), 1)
                    pool.wait_ge(S("idx1"), i * 2 + u + 1)
                    pool.sem_inc(S("gather_go"), 1)
                    pool.indirect_dma_start(out=qg[:, u, :], out_offset=None, in_=v_table[:, :],
                                            in_offset=bass.IndirectOffsetOnAxis(ap=idx_st[:, u, :], axis=0)
                                            ).then_inc(S(f"v_in{u}"), 16)

            pool.wait_ge(S("slots_ready"), 2)
            pool.wait_ge(S("h_done"), CH // G4 + 1)
            for u in range(2):
                pool.wait_ge(S(f"st_x{u}"), 32 * len(range(u, NT, 2)))
            for half in range(2):
                with pool.Fori(0, QUADS) as i:
                    for w in range(2):
                        pr = i * 2 + w + half * 2 * QUADS
                        pool.wait_ge(S("m_done"), pr + 1)
                        pool.tensor_copy(out=idx_st[:, 2 * w:2 * w + 2, 0], in_=gidx[:, 1, ds(i * 4 + 2 * w, 2)]
                                         ).then_inc(S("idx2"), 1)
                        pool.wait_ge(S("idx2"), pr + 1)
                        pool.sem_inc(S("gather_go"), 1)
                        for u in range(2):
                            pool.indirect_dma_start(
                                out=xg[:, w, u, :, :].rearrange("p j f -> p (j f)"), out_offset=None,
                                in_=x_table[half][:, :],
                                in_offset=bass.IndirectOffsetOnAxis(ap=idx_st[:, 2 * w + u, :], axis=0)
                            ).then_inc(S(f"x_in{w}"), 16)

        @block.scalar
        def _(act):
            link = Chain(act, "act_chain")
            for i, name in enumerate(("L0_gnn_ln1_g", "L0_gnn_ln1_b", "L0_gnn_ln2_g", "L0_gnn_ln2_b")):
                act.dma_start(lnp[:, i, :], A[name].rearrange("(k p) -> p k", p=P), allow_slow_non_contiguous=True).then_inc(S("ld_small"), 16)
            act.dma_start(b1col[:, :], A["L0_gnn_b1"].rearrange("(k p) -> p k", p=P), allow_slow_non_contiguous=True).then_inc(S("ld_small"), 16)
            act.dma_start(WO[:, :, :], A["L0_gnn_Wo"].rearrange("(k p) n -> p k n", p=P)).then_inc(S("ld_wo"), 16)
            small_loads = [
                (wf1[:, :], A["L1_gnn_Wf1"]), (bf1[:, :], A["L1_gnn_bf1"].rearrange("(p a) -> p a", a=1)),
                (win[:, 0, :], A["L1_gnn_W_in2f_s"]), (win[:, 1, :], A["L1_gnn_W_in2f_v"]),
                (w1sv[:, 0, :, :], A["L1_gnn_W1_s"].rearrange("(f a) c -> f a c", a=2)),
                (w1sv[:, 1, :, :], A["L1_gnn_W1_v"].rearrange("(f a) c -> f a c", a=2)),
                (w2sv[:, 0, :], A["L1_gnn_W2_s"]), (w2sv[:, 1, :], A["L1_gnn_W2_v"]),
            ]
            for dst, src in small_loads:
                act.dma_start(dst, src).then_inc(S("ld_l1"), 16)

            def sqrt_var(k):
                act.wait_ge(S("ln_stats"), k)
                act.wait_ge(S("consts"), 7)
                act.activation(std[:, :], mv[:, :, 1], ACT.Sqrt, bias=eps[:, :]).then_inc(S("ln_std"), 1)

            def evac_ht(g, first, done, total, scale_bias):
                for k in range(g):
                    act.wait_ge(S(first), k + 1)
                    kw = scale_bias(k)
                    act.activation(ht[:, k, :], pair(2 * (k % 2))[:, 0:NP], ACT.Identity, **kw).then_inc(S(done), 1)

            act.wait_ge(S("rsq_done"), 1)
            act.activation(rnorm[:, 0, :], rnorm[:, 0, :], ACT.Sqrt).then_inc(S("rnorm_done"), 1)
            sqrt_var(1)
            sqrt_var(2)
            act.wait_ge(S("ld_small"), 80)
            evac_ht(KT, "t1_ps", "ht1", KT, lambda k: dict(scale=lnp[:, 0, k:k + 1], bias=lnp[:, 1, k:k + 1]))

            with act.Fori(0, CH // 2) as i:
                for u in range(2):
                    c = i * 2 + u
                    act.wait_ge(S("ot_ps"), c + 3)
                    act.wait_ge(S("kg_mm"), c + 1)
                    act.activation(OTf[:, u, :], PS[:, 7, 0:P], ACT.Copy).then_inc(S("ot_f"), 1)
                    act.activation(OTb[:, ds(c * P, P)], PS[:, 7, 0:P], ACT.Copy).then_inc(S("ot_b"), 1)

            act.wait_ge(S("shifted"), 1)
            act.activation(logit[:, :, :], logit[:, :, :], ACT.Exp).then_inc(S("exp_done"), 1)

            for k in range(KT):
                act.wait_ge(S("t2_ps"), k + 1)
                act.activation(ht[:, k, :], pair(6)[:, 0:NP] if k % 2 else pair(4)[:, 0:NP], ACT.Copy).then_inc(S("ht2"), 1)
            sqrt_var(3)
            act.wait_ge(S("wo_mm"), NT)
            evac_ht(KT, "t3_ps", "ht3", KT, lambda k: dict(scale=lnp[:, 2, k:k + 1], bias=lnp[:, 3, k:k + 1]))
            for f in range(FT):
                act.wait_ge(S("w1_mm"), f + 1)
                act.activation(gelu_t[:, f, :].rearrange("p (a n) -> p a n", a=2),
                               PS[:, 4 + 2 * (f % 2):6 + 2 * (f % 2), 0:NH], ACT.Gelu,
                               bias=b1col[:, f:f + 1]).then_inc(S("gelu"), 1)
            sqrt_var(4)
            evac_ht(4, "t4_ps", "ht4", KT, lambda k: dict())

            act.wait_ge(S("ld_l1"), 16 * len(small_loads))
            with act.Fori(0, CH // G4 // 3) as i3:
                for r in range(3):
                    g = i3 * 3 + r
                    act.wait_ge(S("z_mm"), g + 2)
                    act.wait_ge(S("h_done"), g + 1)
                    act.activation(zed[:, 0, :], PS[:, 2, :], ACT.Identity, bias=bf1[:, :]).then_inc(S("z_sb"), 1)
                    act.wait_ge(S("zab_done"), g + 1)
                    act.activation(zln[:, 0, :], zab[:, 0, :], ACT.Exp).then_inc(S("z_exp"), 1)
                    act.wait_ge(S("z_exp"), g + 1)
                    act.activation(zln[:, 1, :], zln[:, 0, :], ACT.Ln, bias=1.0).then_inc(S("z_ln"), 1)

            for half in range(2):
                with act.Fori(0, QUADS) as i:
                    for w in range(2):
                        pr = i * 2 + w + half * 2 * QUADS
                        act.wait_ge(S("w_mm"), pr + 1)
                        act.activation(hs[:, w, :], h_t[:, ds((i * 4 + 2 * w) * P, 2 * P)], ACT.Copy
                                       ).then_inc(S("hs_done"), 1)

            for m in range(NCOMP):
                act.wait_ge(S("t5_ps"), m + 1)
                act.activation(agg_t[:, m, :], pair(2 * (m % 2))[:, 0:NP], ACT.Copy, scale=COMP_SCALE[m]
                               ).then_inc(S("at_sb"), 1)
            act.wait_ge(S("s_mm"), 1)
            act.activation(s_z.rearrange("p (a n) -> p a n", a=2), PS[:, 4:6, 0:NH], ACT.Copy).then_inc(S("sz"), 1)
            act.wait_ge(S("s_abs"), 1)
            link(act.activation(s_t[:, :], s_e[:, :], ACT.Exp))
            act.activation(s_e[:, :], s_t[:, :], ACT.Ln, bias=1.0).then_inc(S("s_ln"), 1)
            for i in range(3):
                act.wait_ge(S("v_mm"), i + 1)
                act.activation(v_t[:, i, :].rearrange("p (a n) -> p a n", a=2),
                               PS[:, 6:8, 0:NH] if i % 2 == 0 else PS[:, 0:2, 0:NH], ACT.Copy).then_inc(S("v_sb"), 1)

        @block.vector
        def _(dve):
            link = Chain(dve, "dve_chain")
            for name in ("prod_done", "mask_t", "kg_mm", "max_done", "mask_done", "msg_done", "agg_mm",
                         "m_done", "w_mm", "agg1_mm", "ot_ps"):
                dve.sem_inc(S(name), 2)
            for name in ("ot_b", "h_done", "ft_t", "z_mm", "ft_sb", "z_sb"):
                dve.sem_inc(S(name), 1)

            dve.wait_ge(S("consts"), 7)
            dve.wait_ge(S("ld_keys"), 32)

            def bucket(k):
                link(dve.tensor_copy(out=keyf[:, k, :], in_=keyi[:, k, :]))
                dve.memset(ge[:, 0, :], 1.0)
                link(dve.memset(ge[:, NT, :], 0.0))
                for t in range(1, NT):
                    ins = dve.tensor_scalar(ge[:, t, :], keyf[:, k, :], float(P * t), None, ALU.is_ge)
                    link(ins)
                link(dve.tensor_tensor(out=in_b, in0=ge[:, 0:NT, :], in1=ge[:, 1:NT + 1, :], op=ALU.subtract))
                for t in range(NT):
                    link(dve.tensor_tensor_scan(out=cum[:, t, :], data0=in_b[:, t, :], data1=zer[0:EP, 0:EC],
                                                initial=0.0, op0=ALU.add, op1=ALU.add))
                dve.sem_inc(S("counts"), 1)
                dve.wait_ge(S("prefix"), k + 1)
                link(dve.tensor_copy(out=small[:, k, 0:2, :], in_=PS[:, 0, 0:2 * NT].rearrange("p (a t) -> p a t", a=2)))
                link(dve.tensor_scalar(small[:, k, 2, :], small[:, k, 1, :], float(P - 1), None, ALU.add))
                link(dve.tensor_copy(out=small_i[:, k, :], in_=small[:, k, 2, :]))
                link(dve.tensor_scalar(small_i[:, k, :], small_i[:, k, :], 7, None, ALU.arith_shift_right))
                link(dve.tensor_copy(out=small[:, k, 3, :], in_=small_i[:, k, :]))
                link(dve.memset(start[:, k, 0:1], 0.0))
                link(dve.tensor_tensor_scan(out=start[:, k, 1:NT], data0=small[:, k, 3, 0:NT - 1],
                                            data1=zer[:, 0:NT - 1], initial=0.0, op0=ALU.add, op1=ALU.add))
                link(dve.scalar_tensor_tensor(out=offs[:, k, :], in0=start[:, k, :], scalar=float(P),
                                              in1=small[:, k, 0, :], op0=ALU.mult, op1=ALU.add))
                link(dve.tensor_scalar(offs[:, k, :], offs[:, k, :], -1.0, None, ALU.add))
                for t in range(NT):
                    link(dve.scalar_tensor_tensor(out=cum[:, t, :], in0=cum[:, t, :], scalar=offs[0:EP, k, t:t + 1],
                                                  in1=in_b[:, t, :], op0=ALU.add, op1=ALU.mult))
                for t in range(1, NT):
                    link(dve.tensor_tensor(out=cum[:, 0, :], in0=cum[:, 0, :], in1=cum[:, t, :], op=ALU.add))
                link(dve.tensor_copy(out=pos[:, k, :], in_=cum[:, 0, :]))
                link(dve.tensor_scalar(tilef[:, k, :], iota_c[:, :], start[:, k, 1:2], None, ALU.is_ge))
                for t in range(2, NT):
                    link(dve.scalar_tensor_tensor(out=tilef[:, k, :], in0=iota_c[:, :], scalar=start[:, k, t:t + 1],
                                                  in1=tilef[:, k, :], op0=ALU.is_ge, op1=ALU.add))
                dve.tensor_copy(out=tilei[:, k, :], in_=tilef[:, k, :]).then_inc(S("tiles"), 1)
                link(dve.tensor_copy(out=pack[k][:, :, 0], in_=keyf[:, k, :]))
                link(dve.tensor_copy(out=pack[k].bitcast(I32)[:, :, 1], in_=keyi[:, 1 - k, :]))

            dve.wait_ge(S("ld_r"), 32)
            link(dve.tensor_tensor(out=rsq, in0=raw_r, in1=raw_r, op=ALU.mult))
            link(dve.tensor_reduce(out=rnorm[:, 0, :], in_=rsq, axis=X_AXIS, op=ALU.add))
            dve.sem_inc(S("rsq_done"), 1)
            bucket(0)
            dve.wait_ge(S("ld_bias"), 32)
            link(dve.tensor_tensor(out=pack[0][:, :, 2:W0], in0=raw0[:, 0, :, :], in1=raw0[:, 1, :, :], op=ALU.add))
            dve.sem_inc(S("packed"), 1)

            def row_stats(src):
                for t in range(NT):
                    link(dve.bn_stats(stats[:, t, :], src[:, t, :]))
                    ins = dve.bn_aggr(mv[:, t, :], stats[:, t, :])
                    if t < NT - 1:
                        link(ins)
                ins.then_inc(S("ln_stats"), 1)

            def normalise(k, src, dst, done=None):
                dve.wait_ge(S("ln_std"), k)
                link(dve.reciprocal(rstd[:, :], std[:, :]))
                for t in range(NT):
                    ins = dve.tensor_scalar(dst[:, t, :], src[:, t, :], mv[:, t, 0:1], rstd[:, t:t + 1],
                                            ALU.subtract, ALU.mult)
                    if done:
                        ins.then_inc(S(done), 1)
                    else:
                        link(ins)

            dve.wait_ge(S("ld_x"), 16 * NT)
            row_stats(X)
            normalise(1, X, h0)
            link(dve.tensor_scalar(H0[:, :], H0[:, :], 0.0, None, ALU.max))
            row_stats(h0)
            normalise(2, h0, hn, "hn1")

            bucket(1)
            dve.wait_ge(S("ld_f"), 16)
            dve.wait_ge(S("rnorm_done"), 1)
            link(dve.reciprocal(rnorm[:, 0, :], rnorm[:, 0, :]))
            link(dve.tensor_tensor(out=pack[1][:, :, 3:6], in0=raw_r,
                                   in1=rnorm[:, 0, :].unsqueeze(2).to_broadcast([EP, EC, 3]), op=ALU.mult))
            link(dve.tensor_copy(out=pack[1][:, :, 2], in_=rnorm[:, 1, :]))
            dve.sem_inc(S("packed"), 1)

            dve.wait_ge(S("ld_brow"), 16)
            for t in range(NT):
                for j in range(3):
                    n = 3 * t + j
                    dve.wait_ge(S("qkv_mm"), n + 1)
                    if t >= 2 and j == 0:
                        dve.wait_ge(S(f"st_qv{t % 2}"), 32 * (t // 2))
                    dst = (qst[:, t % 2, 0, :], K_sb[:, t, :], qst[:, t % 2, 1, :])[j]
                    ins = dve.tensor_tensor(out=dst, in0=PS[:, 4 + n % 4, :], in1=brow[:, j * D:(j + 1) * D], op=ALU.add)
                    ins.then_inc(S("qkv_sb"), 1)
                dve.wait_ge(S("qkv_sb"), 3 * t + 3)
                dve.sem_inc(S("qv_rows"), 1)

            for k in range(2):
                dve.wait_ge(S(f"ld_slots{k}"), 16)
                link(dve.scalar_tensor_tensor(out=local[:, k, :], in0=tilef[:, k, :], scalar=float(-P),
                                              in1=slots[k][:, :, 0], op0=ALU.mult, op1=ALU.add))
                link(dve.tensor_copy(out=gidx[:, k, :], in_=slots[k][:, :, :].bitcast(I32)[:, :, 1]))
                dve.sem_inc(S("slots_ready"), 1)

            def onehot(c, u):
                dve.wait_ge(S("ot_ps"), c + 1)
                dve.tensor_scalar(O[:, u, :], iota_n[:, :], local[:, 0, ds(c, 1)], None, ALU.is_equal).then_inc(S("oh_done"), 1)
                dve.wait_ge(S("mask_done"), c + 1)
                dve.tensor_scalar(pen[:, u, :], iota_n[:, :], local[:, 0, ds(c, 1)], -BIG, ALU.not_equal, ALU.mult
                                  ).then_inc(S("pen_done"), 1)

            def logits(c, u, turn):
                dve.wait_ge(S(f"q_in{u}"), turn * 16 + 16)
                dve.wait_ge(S("kg_mm"), c + 3)
                dve.tensor_tensor(out=msg[:, u, :], in0=PS[:, 4 + u, :], in1=qg[:, u, :], op=ALU.mult
                                  ).then_inc(S("prod_done"), 1)
                dve.wait_ge(S("prod_done"), c + 3)
                dve.tensor_reduce(out=araw[:, u, :], in_=msg[:, u, :].rearrange("p (h d) -> p h d", h=H),
                                  axis=X_AXIS, op=ALU.add).then_inc(S("red_done"), 1)
                dve.wait_ge(S("red_done"), c + 1)
                dve.scalar_tensor_tensor(out=logit[:, ds(c, 1), :].rearrange("p a h -> p (a h)"), in0=araw[:, u, :],
                                         scalar=float(D) ** -0.5,
                                         in1=slots0[:, ds(c, 1), 2:W0].rearrange("p a h -> p (a h)"),
                                         op0=ALU.mult, op1=ALU.add).then_inc(S("logit_done"), 1)

            def chunk_max(c, u):
                dve.wait_ge(S("mask_t"), c + 3)
                dve.tensor_reduce(out=cmax[:, ds(c, 1), :].rearrange("p a h -> p (a h)"),
                                  in_=pair(2 * u).rearrange("p (h n) -> p h n", h=H),
                                  axis=X_AXIS, op=ALU.max).then_inc(S("max_done"), 1)

            onehot(0, 0)
            logits(0, 0, 0)
            onehot(1, 1)
            logits(1, 1, 0)
            with dve.Fori(1, CH // 2) as i:
                for u in range(2):
                    onehot(i * 2 + u, u)
                    logits(i * 2 + u, u, i)
                    chunk_max(i * 2 + u - 2, u)
            chunk_max(CH - 2, 0)
            chunk_max(CH - 1, 1)
            dve.wait_ge(S("max_done"), CH + 2)

            for t in range(NT):
                link(dve.tensor_scalar(eqt[:, t, :], tilef[:, 0, :], float(t), None, ALU.is_equal))
            for t in range(NT):
                link(dve.tensor_scalar(zer[:, :], eqt[:, t, :], 1.0, BIG, ALU.subtract, ALU.mult))
                link(dve.tensor_tensor(out=mc[:, :, :], in0=cmax[:, :, :],
                                       in1=zer[:, :].unsqueeze(2).to_broadcast([P, CH, H]), op=ALU.add))
                link(dve.tensor_reduce(out=nmax[:, t, :], in_=mc[:, :, :].rearrange("p c h -> p h c"),
                                       axis=X_AXIS, op=ALU.max))
            for t in range(NT):
                dst = cmax if t else mc
                link(dve.tensor_tensor(out=dst[:, :, :], in0=nmax[:, t, :].unsqueeze(1).to_broadcast([P, CH, H]),
                                       in1=eqt[:, t, :].unsqueeze(2).to_broadcast([P, CH, H]), op=ALU.mult))
                if t:
                    link(dve.tensor_tensor(out=mc[:, :, :], in0=mc[:, :, :], in1=cmax[:, :, :], op=ALU.add))
            for part in range(3):
                link(dve.tensor_copy(out=mc3[:, :, part, :], in_=mc[:, :, :]))
                if part < 2:
                    link(dve.tensor_tensor(out=mc[:, :, :], in0=mc[:, :, :], in1=mc3[:, :, part, :], op=ALU.subtract))
            dve.sem_inc(S("mc_done"), 1)
            for b in range(CH // QB):
                dve.wait_ge(S("mx_mm"), QB * (b + 1))
                for part in range(3):
                    lg = logit[:, QB * b:QB * (b + 1), :]
                    mx = PS[:, b, 0:QB * 3 * H].rearrange("p (c a h) -> p c a h", a=3, h=H)[:, :, part, :]
                    link(dve.tensor_tensor(out=lg, in0=lg, in1=mx, op=ALU.subtract))
            dve.sem_inc(S("shifted"), 1)
            dve.wait_ge(S("exp_done"), 1)

            with dve.Fori(0, CH // 2) as i:
                for u in range(2):
                    c = i * 2 + u
                    dve.wait_ge(S("agg_mm"), c + 1)
                    dve.tensor_scalar(O[:, u, :], iota_n[:, :], local[:, 0, ds(c, 1)], None, ALU.is_equal
                                      ).then_inc(S("oh2_done"), 1)
                    dve.wait_ge(S(f"v_in{u}"), i * 16 + 16)
                    dve.tensor_tensor(out=msg[:, u, :].rearrange("p (h d) -> p h d", h=H),
                                      in0=qg[:, u, :].rearrange("p (h d) -> p h d", h=H),
                                      in1=logit[:, ds(c, 1), :].rearrange("p a h -> p (a h)").unsqueeze(2).to_broadcast([P, H, DH]),
                                      op=ALU.mult).then_inc(S("msg_done"), 1)

            dve.wait_ge(S("agg_closed"), 1)
            link(dve.tensor_copy(out=den[:, 0, :], in_=PS[:, 5, 0:NT * H]))
            link(dve.scalar_tensor_tensor(out=den[:, 1, :], in0=den[:, 0, :], scalar=0.0, in1=den[:, 0, :],
                                          op0=ALU.is_equal, op1=ALU.add))
            link(dve.reciprocal(den[:, 0, :], den[:, 1, :]))
            for t in range(NT):
                dve.tensor_tensor(out=hn[:, t, :].rearrange("p (h d) -> p h d", h=H),
                                  in0=PS[:, t, :].rearrange("p (h d) -> p h d", h=H),
                                  in1=den[:, 0, t * H:(t + 1) * H].unsqueeze(2).to_broadcast([P, H, DH]),
                                  op=ALU.mult).then_inc(S("att_sb"), 1)
            dve.wait_ge(S("ld_b2rows"), 32)
            for t in range(NT):
                link(dve.tensor_tensor(out=h0[:, t, :], in0=h0[:, t, :], in1=brow[:, 0:D], op=ALU.add))
            for t in range(NT):
                dve.wait_ge(S("wo_mm"), t + 1)
                link(dve.tensor_tensor(out=h0[:, t, :], in0=PS[:, t % 4, :], in1=h0[:, t, :], op=ALU.add))
                dve.sem_inc(S("h1_sb"), 1)
            row_stats(h0)
            dve.wait_ge(S("t2_ps"), KT)
            normalise(3, h0, hn, "hn3")
            for t in range(NT):
                link(dve.tensor_tensor(out=h0[:, t, :], in0=h0[:, t, :], in1=brow[:, D:2 * D], op=ALU.add))
                link(dve.tensor_tensor(out=X[:, t, :], in0=h0[:, t, :], in1=X[:, t, :], op=ALU.add))
            for t in range(NT):
                dve.wait_ge(S("w2_mm"), t + 1)
                link(dve.tensor_tensor(out=X[:, t, :], in0=PS[:, t % 4, :], in1=X[:, t, :], op=ALU.add))
                dve.sem_inc(S("x1_sb"), 1)

            row_stats(X)
            dve.wait_ge(S("t3_ps"), KT)
            normalise(4, X, hn)
            for t in range(NT):
                dve.tensor_scalar(hn[:, t, :], hn[:, t, :], 0.0, None, ALU.max).then_inc(S("hn4"), 1)
            dve.wait_ge(S("hn4"), NT)
            for t in range(NT):
                dve.wait_ge(S("xin_mm"), t + 1)
                if t >= 2:
                    dve.wait_ge(S(f"st_x{t % 2}"), 32 * (t // 2))
                else:
                    dve.wait_ge(S("xin_mm"), NT)
                for h in range(2):
                    link(dve.tensor_copy(out=xst[:, t % 2, h, :, :],
                                         in_=PS[:, XB(t), :].rearrange("p (j h f) -> p h j f", j=4, h=2)[:, h, :, :]))
                dve.sem_inc(S("x_rows"), 1)

            dve.wait_ge(S("ld_l1"), 16 * 8)
            dve.wait_ge(S("ld_wf2"), 32)
            for h in range(2):
                for b, at in enumerate((2 * C, 0, 1, 2 * C + 1)):
                    at += 2 * HF * h
                    for dst, src in ((wf2, wfr), (bf2, bfraw)):
                        link(dve.tensor_copy(out=dst[:, h, b * HF:(b + 1) * HF], in_=src[:, at:at + 2 * HF - 1:2]))

            dve.wait_ge(S("t4_ps"), KT)
            with dve.Fori(0, CH // G4) as g:
                dve.wait_ge(S("ft_t"), g + 1)
                dve.tensor_copy(out=fs[:, 0, :].rearrange("p (a f) -> p a f", a=G4),
                                in_=slots1[:, ds(g * G4, G4), 6:W1]).then_inc(S("fs_done"), 1)
                dve.wait_ge(S("ft_t"), g + 2)
                dve.wait_ge(S("z_mm"), g + 1)
                dve.tensor_copy(out=ft[0:NRBF, 0, :], in_=PS[0:NRBF, 3, :]).then_inc(S("ft_sb"), 1)
                dve.wait_ge(S("z_sb"), g + 2)
                dve.scalar_tensor_tensor(out=zab[:, 0, :], in0=zed[:, 0, :], scalar=-1.0, in1=zed[:, 0, :],
                                         op0=ALU.mult, op1=ALU.min).then_inc(S("zab_done"), 1)
                dve.tensor_scalar(zab[:, 1, :], zed[:, 0, :], 0.0, -LOG2, ALU.max, ALU.add).then_inc(S("zrelu"), 1)
                dve.wait_ge(S("zrelu"), g + 1)
                dve.wait_ge(S("z_ln"), g + 1)
                dve.tensor_tensor(out=h_t[:, ds(g * G4 * P, G4 * P)], in0=zln[:, 1, :], in1=zab[:, 1, :], op=ALU.add
                                  ).then_inc(S("h_done"), 1)
            dve.wait_ge(S("h_done"), CH // G4 + 1)

            for half in range(2):
                chain = LoopChain(dve, f"l1_chain{half}", 2 * 5)
                with dve.Fori(0, QUADS) as i:
                    chain.turn(i)
                    for w in range(2):
                        pr = i * 2 + w + half * 2 * QUADS
                        c = i * 4 + 2 * w
                        xv = xg[:, w, :, 1:4, :]
                        xs = xg[:, w, :, 0, :]
                        uu = slots1[:, ds(c, 2), 3:6].unsqueeze(3).to_broadcast([P, 2, 3, HF])
                        W = PS[:, 5 + w, :].rearrange("p (u b f) -> p u b f", u=2, b=4)
                        dve.wait_ge(S("agg1_mm"), pr + 1)
                        for u in range(2):
                            dve.tensor_scalar(O[:, 2 * w + u, :], iota_n[:, :], local[:, 1, ds(c + u, 1)],
                                              slots1[:, ds(c + u, 1), 2], ALU.is_equal, ALU.mult)
                        dve.wait_ge(S(f"x_in{w}"), i * 32 + 32 + half * 32 * QUADS)
                        chain(dve.tensor_tensor(out=xvu, in0=xv, in1=uu, op=ALU.mult))
                        chain(dve.tensor_tensor(out=dotu, in0=xvu[:, :, 0, :], in1=xvu[:, :, 1, :], op=ALU.add))
                        chain(dve.tensor_tensor(out=dotu, in0=dotu, in1=xvu[:, :, 2, :], op=ALU.add))
                        dve.wait_ge(S("w_mm"), pr + 3)
                        chain(dve.tensor_tensor(out=M[:, w, :, 0:2, :], in0=W[:, :, 0:2, :],
                                                in1=xs.unsqueeze(2).to_broadcast([P, 2, 2, HF]), op=ALU.mult))
                        dve.tensor_tensor(out=M[:, w, :, 2, :], in0=W[:, :, 2, :], in1=dotu, op=ALU.mult)
                        dve.tensor_tensor(out=M[:, w, :, 3:6, :],
                                          in0=W[:, :, 3, :].unsqueeze(2).to_broadcast([P, 2, 3, HF]), in1=xv, op=ALU.mult)
                        chain(dve.tensor_tensor(out=M[:, w, :, 6:9, :],
                                                in0=M[:, w, :, 0, :].unsqueeze(2).to_broadcast([P, 2, 3, HF]),
                                                in1=uu, op=ALU.mult))
                        dve.sem_inc(S("m_done"), 1)
                dve.wait_ge(S("agg1_closed"), half + 1)
                for t in range(NT):
                    link(dve.tensor_copy(out=agg1[:, t, :, HF * half:HF * (half + 1)],
                                         in_=PS[:, t, :].rearrange("p (m f) -> p m f", m=NCOMP)))
                dve.sem_inc(S("agg1_sb"), 1)

            dve.wait_ge(S("sz"), 1)
            dve.scalar_tensor_tensor(out=s_e[:, :], in0=s_z[:, :], scalar=-1.0, in1=s_z[:, :],
                                     op0=ALU.mult, op1=ALU.min).then_inc(S("s_abs"), 1)
            link(dve.tensor_scalar(s_z[:, :], s_z[:, :], 0.0, -LOG2, ALU.max, ALU.add))
            dve.wait_ge(S("s_ln"), 1)
            dve.tensor_tensor(out=s_z[:, :], in0=s_z[:, :], in1=s_e[:, :], op=ALU.add).then_inc(S("s_sb"), 1)
            for t in range(NT):
                dve.wait_ge(S("out_mm"), t + 1)
                link(dve.scalar_tensor_tensor(out=X[:, t, 0:C], in0=PS[:, OB(t), 0:C], scalar=RC, in1=X[:, t, 0:C],
                                              op0=ALU.mult, op1=ALU.add))
                xv_out = X[:, t, C:D].rearrange("p (d i) -> p i d", i=3)
                link(dve.scalar_tensor_tensor(out=xv_out, in0=PS[:, OB(t), C:D].rearrange("p (i d) -> p i d", i=3),
                                              scalar=RC, in1=xv_out, op0=ALU.mult, op1=ALU.add))
                dve.sem_inc(S("out_rows"), 1)

        @block.tensor
        def _(pe):
            pe.wait_ge(S("consts"), 7)

            def bucket_sums(k):
                pe.wait_ge(S("counts"), k + 1)
                pe.matmul(PS[:, 0, 0:NT], tri[0:EP, :], cum[:, :, EC - 1], start=True, stop=True)
                pe.matmul(PS[:, 0, NT:2 * NT], ones[0:EP, :], cum[:, :, EC - 1], start=True, stop=True
                          ).then_inc(S("prefix"), 1)

            bucket_sums(0)

            def transposes(groups, ready, done, freed, src, banks):
                pe.wait_ge(S(ready), NT)
                for k in range(groups):
                    if k >= 2:
                        pe.wait_ge(S(freed), k - 1)
                    for t in range(NT):
                        ins = pe.transpose(pair(banks[k % 2])[:, t * P:(t + 1) * P], src(k, t), ident[:, :])
                    ins.then_inc(S(done), 1)

            transposes(KT, "hn1", "t1_ps", "ht1", lambda k, t: hn[:, t, k * P:(k + 1) * P], (0, 2))
            pe.wait_ge(S("ht1"), KT)
            bucket_sums(1)
            pe.wait_ge(S("ld_wqkv"), 16)
            for t in range(NT):
                for j in range(3):
                    n = 3 * t + j
                    if n >= 4:
                        pe.wait_ge(S("qkv_sb"), n - 3)
                    for k in range(KT):
                        ins = pe.matmul(PS[:, 4 + n % 4, :], ht[:, k, t * P:(t + 1) * P], wqkv[:, k, j * D:(j + 1) * D],
                                        start=(k == 0), stop=(k == KT - 1))
                    ins.then_inc(S("qkv_mm"), 1)

            def one_hot_t(c, u):
                pe.wait_ge(S("oh_done"), c + 1)
                pe.wait_ge(S("ot_b"), c + 1)
                pe.transpose(PS[:, 7, 0:P], O[:, u, :], ident[:, :]).then_inc(S("ot_ps"), 1)

            def mask_transposes(c, u):
                pe.wait_ge(S("mask_done"), c + 3)
                pe.wait_ge(S("max_done"), c + 1)
                for h in range(H):
                    ins = pe.transpose(pair(2 * u)[:, h * P:(h + 1) * P], masked[:, u, h, :], ident[:, :])
                ins.then_inc(S("mask_t"), 1)

            def k_gather(c, u):
                tile = pe.value_load(tilei[0:1, 0, ds(c, 1)], min_val=0, max_val=NT - 1)
                pe.wait_ge(S("ot_f"), c + 1)
                pe.wait_ge(S("prod_done"), c + 1)
                pe.matmul(PS[:, 4 + u, :], OTf[:, u, :], K_sb[:, ds(tile, 1), :].rearrange("p a n -> p (a n)"),
                          start=True, stop=True).then_inc(S("kg_mm"), 1)

            pe.wait_ge(S("qkv_sb"), 3 * NT)
            pe.wait_ge(S("slots_ready"), 1)
            pe.wait_ge(S("tiles"), 1)
            one_hot_t(0, 0)
            k_gather(0, 0)
            one_hot_t(1, 1)
            k_gather(1, 1)
            mask_transposes(0, 0)
            with pe.Fori(1, CH // 2) as i:
                for u in range(2):
                    one_hot_t(i * 2 + u, u)
                    k_gather(i * 2 + u, u)
                    mask_transposes(i * 2 + u - 1, 1 - u)
            mask_transposes(CH - 1, 1)

            pe.wait_ge(S("mc_done"), 1)
            pe.wait_ge(S("ot_b"), CH + 1)
            for b in range(CH // QB):
                with pe.Fori(0, QB) as j:
                    pe.matmul(PS[:, b, ds(j * 3 * H, 3 * H)], OTb[:, ds((j + b * QB) * P, P)],
                              mc3[:, ds(j + b * QB, 1), :, :].rearrange("p c a h -> p (c a h)"),
                              start=True, stop=True).then_inc(S("mx_mm"), 1)

            def open_close(banks, start):
                for b in banks:
                    ins = pe.matmul(PS[:, b, :], zeros_l, zeros_r, start=start, stop=not start)
                return ins

            zeros_l, zeros_r = zero_w[:, 0:P], zero_w[:, :]
            pe.wait_ge(S("shifted"), 1)
            open_close(range(6), True)
            with pe.Fori(0, CH // 2) as i:
                for u in range(2):
                    c = i * 2 + u
                    tile = pe.value_load(tilei[0:1, 0, ds(c, 1)], min_val=0, max_val=NT - 1)
                    pe.wait_ge(S("msg_done"), c + 3)
                    pe.matmul(PS[:, ds(tile, 1), :].rearrange("p a n -> p (a n)"), O[:, u, :], msg[:, u, :],
                              start=False, stop=False)
                    pe.matmul(PS[:, 5, ds(tile * H, H)], O[:, u, :],
                              logit[:, ds(c, 1), :].rearrange("p a h -> p (a h)"),
                              start=False, stop=False).then_inc(S("agg_mm"), 1)
            open_close(range(6), False).then_inc(S("agg_closed"), 1)

            pe.wait_ge(S("att_sb"), NT)
            transposes(KT, "att_sb", "t2_ps", "ht2", lambda k, t: hn[:, t, k * P:(k + 1) * P], (4, 6))
            pe.wait_ge(S("ht2"), KT)
            pe.wait_ge(S("ld_wo"), 16)
            for t in range(NT):
                if t >= 4:
                    pe.wait_ge(S("h1_sb"), t - 3)
                for k in range(KT):
                    ins = pe.matmul(PS[:, t % 4, :], ht[:, k, t * P:(t + 1) * P], WO[:, k, :],
                                    start=(k == 0), stop=(k == KT - 1))
                ins.then_inc(S("wo_mm"), 1)
            pe.wait_ge(S("h1_sb"), NT)
            transposes(KT, "hn3", "t3_ps", "ht3", lambda k, t: hn[:, t, k * P:(k + 1) * P], (0, 2))
            pe.wait_ge(S("ht3"), KT)
            pe.wait_ge(S("ld_w1"), 16)
            for f in range(FT):
                if f >= 2:
                    pe.wait_ge(S("gelu"), f - 1)
                for a in range(2):
                    for k in range(KT):
                        ins = pe.matmul(PS[:, 4 + 2 * (f % 2) + a, 0:NH], w1[:, k, f * P:(f + 1) * P],
                                        ht[:, k, a * NH:(a + 1) * NH], start=(k == 0), stop=(k == KT - 1))
                ins.then_inc(S("w1_mm"), 1)
            pe.wait_ge(S("gelu"), FT)
            pe.wait_ge(S("ld_w2"), 16)
            for t in range(NT):
                if t >= 4:
                    pe.wait_ge(S("x1_sb"), t - 3)
                for f in range(FT):
                    ins = pe.matmul(PS[:, t % 4, :], gelu_t[:, f, t * P:(t + 1) * P], w2[:, f, :],
                                    start=(f == 0), stop=(f == FT - 1))
                ins.then_inc(S("w2_mm"), 1)

            pe.wait_ge(S("x1_sb"), NT)
            transposes(4, "hn4", "t4_ps", "ht4",
                       lambda j, t: hn[:, t, 0:C] if j == 0 else hn[:, t, C + j - 1:D:3], (0, 2))
            pe.wait_ge(S("ht4"), 4)
            pe.wait_ge(S("ld_l1"), 16 * 8)
            for t in range(NT):
                for j in range(4):
                    ins = pe.matmul(PS[:, XB(t), j * C:(j + 1) * C], ht[:, j, t * P:(t + 1) * P],
                                    win[:, min(j, 1), :], start=True, stop=True)
                ins.then_inc(S("xin_mm"), 1)

            pe.wait_ge(S("x_rows"), NT)
            with pe.Fori(0, CH // G4) as g:
                pe.wait_ge(S("fs_done"), g + 1)
                pe.wait_ge(S("ft_sb"), g + 1)
                for a in range(G4):
                    ins = pe.transpose(PS[0:NRBF, 3, a * P:(a + 1) * P], fs[:, 0, a * NRBF:(a + 1) * NRBF], ident[:, :])
                ins.then_inc(S("ft_t"), 1)
                pe.wait_ge(S("ft_sb"), g + 2)
                pe.wait_ge(S("z_sb"), g + 1)
                pe.matmul(PS[:, 2, :], wf1[:, :], ft[0:NRBF, 0, :], start=True, stop=True).then_inc(S("z_mm"), 1)

            pe.wait_ge(S("h_done"), CH // G4 + 1)
            pe.wait_ge(S("tiles"), 2)

            def filters(i, w, half):
                pr = i * 2 + w + half * 2 * QUADS
                pe.wait_ge(S("hs_done"), pr + 1)
                pe.wait_ge(S("m_done"), pr + 1)
                for u in range(2):
                    dst = PS[:, 5 + w, u * 4 * HF:(u + 1) * 4 * HF]
                    pe.matmul(dst, hs[:, w, u * P:(u + 1) * P], wf2[:, half, :], start=True, stop=False)
                    ins = pe.matmul(dst, ones[0:1, :], bf2[:, half, :], start=False, stop=True)
                ins.then_inc(S("w_mm"), 1)

            def scatter(i, w, half):
                pr = i * 2 + w + half * 2 * QUADS
                tiles = [pe.value_load(tilei[0:1, 1, ds(i * 4 + 2 * w + u, 1)], min_val=0, max_val=NT - 1)
                         for u in range(2)]
                pe.wait_ge(S("m_done"), pr + 3)
                for u in range(2):
                    ins = pe.matmul(PS[:, ds(tiles[u], 1), :].rearrange("p a n -> p (a n)"), O[:, 2 * w + u, :],
                                    M[:, w, u, 1:9, :].rearrange("p m f -> p (m f)"), start=False, stop=False)
                ins.then_inc(S("agg1_mm"), 1)

            for half in range(2):
                if half:
                    pe.wait_ge(S("agg1_sb"), half)
                open_close(range(NT), True)
                filters(0, 0, half)
                with pe.Fori(0, QUADS - 1) as i:
                    filters(i, 1, half)
                    scatter(i, 0, half)
                    filters(i + 1, 0, half)
                    scatter(i, 1, half)
                filters(QUADS - 1, 1, half)
                scatter(QUADS - 1, 0, half)
                scatter(QUADS - 1, 1, half)
                open_close(range(NT), False).then_inc(S("agg1_closed"), 1)

            pe.wait_ge(S("agg1_sb"), 2)
            for m in range(NCOMP):
                if m >= 2:
                    pe.wait_ge(S("at_sb"), m - 1)
                for t in range(NT):
                    ins = pe.transpose(pair(2 * (m % 2))[:, t * P:(t + 1) * P], agg1[:, t, m, :], ident[:, :])
                ins.then_inc(S("t5_ps"), 1)
            pe.wait_ge(S("at_sb"), NCOMP)
            for a in range(2):
                for k in range(2):
                    ins = pe.matmul(PS[:, 4 + a, 0:NH], w1sv[:, 0, k, :], agg_t[:, k, a * NH:(a + 1) * NH],
                                    start=(k == 0), stop=(k == 1))
            ins.then_inc(S("s_mm"), 1)
            for i in range(3):
                if i == 2:
                    pe.wait_ge(S("v_sb"), 1)
                b = 6 if i % 2 == 0 else 0
                for a in range(2):
                    for k in range(2):
                        ins = pe.matmul(PS[:, b + a, 0:NH], w1sv[:, 1, k, :], agg_t[:, (5 if k == 0 else 2) + i, a * NH:(a + 1) * NH],
                                        start=(k == 0), stop=(k == 1))
                ins.then_inc(S("v_mm"), 1)
            pe.wait_ge(S("v_sb"), 3)
            pe.wait_ge(S("s_sb"), 1)
            for t in range(NT):
                for j in range(4):
                    lhs = s_z if j == 0 else v_t[:, j - 1, :]
                    ins = pe.matmul(PS[:, OB(t), j * C:(j + 1) * C], lhs[:, t * P:(t + 1) * P], w2sv[:, min(j, 1), :],
                                    start=True, stop=True)
                ins.then_inc(S("out_mm"), 1)


_OUTS = [((625, 512), "float32")]


def kernel(**inputs):
    import numpy as _np
    import concourse.bacc as _bacc
    from concourse import mybir as _mybir
    from concourse.bass_utils import run_bass_kernel_spmd as _run

    nc = _bacc.Bacc("TRN2", target_bir_lowering=False, num_devices=1)
    arrays, args = {}, {}
    for name in inputs:
        a = _np.ascontiguousarray(inputs[name])
        arrays[f"in_{name}_dram"] = a
        args[name] = nc.dram_tensor(f"in_{name}_dram", a.shape, _mybir.dt.from_np(a.dtype), kind="ExternalInput").ap()
    out = nc.dram_tensor("out_0_dram", _OUTS[0][0], _mybir.dt.from_np(_np.dtype(_OUTS[0][1])), kind="ExternalOutput").ap()
    gnn_two_layer_kernel(nc, args, out)
    r = _run(nc, [arrays], core_ids=[0])
    return r.results[0]["out_0_dram"]
```

```python
import concourse.bass as bass
from concourse import mybir
from contextlib import ExitStack


def gnn_two_layer_kernel(nc: bass.Bass, A: dict, out: bass.AP, debug=False):
    F32 = mybir.dt.float32
    I32 = mybir.dt.int32
    BF16 = mybir.dt.bfloat16
    ALU = mybir.AluOpType
    ACT = mybir.ActivationFunctionType
    X_AXIS = mybir.AxisListType.X
    ds = bass.ds

    P = 128
    N, D = A["x"].shape
    E = A["src"].shape[0]
    H = A["edge_attr_8"].shape[1]
    DH = D // H
    NRBF = A["edge_attr_20"].shape[1]
    C = A["L1_gnn_W_in2f_s"].shape[0]
    FD = A["L0_gnn_W1"].shape[1]
    KT = D // P
    FT = FD // P
    NT = -(-N // P)
    NP = NT * P
    NH = NP // 2
    ROWS = [min(P, N - P * t) for t in range(NT)]
    EP = next(p for p in range(P, 0, -1) if E % p == 0)
    EC = E // EP
    CH = (E + NT * (P - 1)) // P
    CH += -CH % 4
    SLOTS = CH * P
    W0 = 2 + H
    W1 = 6 + NRBF
    HF = C // 2
    G4 = 4
    QB = 21
    QUADS = CH // 4
    PENALTY = 1e30
    EPS = 1e-5
    LOG2 = 0.6931471805599453
    Y0 = (4.0 * 3.141592653589793) ** -0.5
    Y1 = (3.0 / (4.0 * 3.141592653589793)) ** 0.5
    RC = C ** -0.5
    R2F = (2 * C) ** -0.5
    NCOMP = 8
    COMP_SCALE = [Y0 * RC * R2F, Y1 * RC * R2F * 3 ** -0.5] + [Y0 * RC * R2F] * 3 + [Y1 * RC * R2F] * 3
    assert CH % QB == 0 and CH % G4 == 0 and QB * 3 * H <= 512 and D == 4 * C

    ctx = ExitStack()
    with ctx:
        def sb(name, shape, dt=F32):
            return ctx.enter_context(nc.sbuf_tensor(name, shape, dt))

        def dram(name, shape, dt=F32):
            return nc.dram_tensor(name, shape, dt, kind="ExternalOutput" if debug else "Internal")

        q_table = dram("q_table", [N, D])
        v_table = dram("v_table", [N, D])
        slots_dram = [dram("slots0_dram", [SLOTS, W0]), dram("slots1_dram", [SLOTS, W1])]
        x_table = [dram(f"x_table{h}", [N, 4 * HF]) for h in range(2)]

        def region(tensor):
            at = [0]

            def carve(width, dt=F32, parts=P):
                words = width if dt != BF16 else width // 2
                a = tensor[0:parts, at[0]:at[0] + words]
                at[0] += words
                assert at[0] <= tensor.shape[1], (at[0], tensor.shape)
                return a if dt == F32 else a.bitcast(dt)
            return carve

        X = sb("X", [P, NT, D])
        H0 = sb("H0", [P, NT * D])
        HN = sb("HN", [P, NT * D])
        BIG = sb("BIG", [P, KT * NP + 2 * FT * D])
        HT, PART1, PART2 = BIG[:, 0:KT * NP], BIG[:, KT * NP:KT * NP + FT * D], BIG[:, KT * NP + FT * D:]
        ARENA = sb("ARENA", [P, FT * NP])
        WO = sb("WO", [P, KT, D])
        h0 = H0[:, :].rearrange("p (t n) -> p t n", t=NT)
        hn = HN[:, :].rearrange("p (t n) -> p t n", t=NT)
        ht = HT.rearrange("p (k n) -> p k n", k=KT)
        wqkv = PART1[:, 0:KT * 3 * D].rearrange("p (k n) -> p k n", k=KT)
        w1 = PART1[:, 0:KT * FD].rearrange("p (k n) -> p k n", k=KT)
        w2 = PART2.rearrange("p (f n) -> p f n", f=FT)
        gelu_t = ARENA[:, :].rearrange("p (f n) -> p f n", f=FT)

        PACK1_AT = FT * D - EC * W1
        W2_EARLY = PACK1_AT // D
        carve = region(PART2[:, 0:PACK1_AT])
        raw0 = carve(2 * EC * H, parts=EP).rearrange("p (a c h) -> p a c h", a=2, h=H)
        raw_r = carve(EC * 3, parts=EP).rearrange("p (c i) -> p c i", i=3)
        rsq = carve(EC * 3, parts=EP).rearrange("p (c i) -> p c i", i=3)
        rnorm = carve(EC * 2, parts=EP).rearrange("p (a c) -> p a c", a=2)
        pack = [carve(EC * W0, parts=EP).rearrange("p (c w) -> p c w", w=W0),
                PART2[0:EP, PACK1_AT:].rearrange("p (c w) -> p c w", w=W1)]
        keyf = carve(2 * EC, parts=EP).rearrange("p (k c) -> p k c", k=2)
        ge = carve((NT + 1) * EC, parts=EP).rearrange("p (t c) -> p t c", c=EC)
        in_b = carve(NT * EC, parts=EP).rearrange("p (t c) -> p t c", c=EC)
        cum = carve(NT * EC, parts=EP).rearrange("p (t c) -> p t c", c=EC)
        carve = region(PART2[:, 0:PACK1_AT])
        OTb = carve(SLOTS, BF16)
        carve = region(ARENA)
        K_sb = carve(NT * D).rearrange("p (t n) -> p t n", t=NT)
        qg = carve(4 * D).rearrange("p (v n) -> p v n", v=4)
        msg = carve(2 * D).rearrange("p (u n) -> p u n", u=2)
        masked = carve(2 * H * P).rearrange("p (u h n) -> p u h n", u=2, h=H)
        qst = carve(2 * 2 * D).rearrange("p (u a n) -> p u a n", u=2, a=2)
        h_t = BIG[:, 0:SLOTS]
        carve = region(HN)
        ft = carve(2 * G4 * P).rearrange("p (r n) -> p r n", r=2)
        zed = carve(2 * G4 * P).rearrange("p (r n) -> p r n", r=2)
        carve = region(H0)
        znab = carve(G4 * P)
        zrelu = carve(2 * G4 * P).rearrange("p (r n) -> p r n", r=2)
        zln = carve(2 * G4 * P).rearrange("p (r n) -> p r n", r=2)
        carve = region(ARENA)
        xin_t = carve(4 * NP).rearrange("p (j n) -> p j n", j=4)
        xst = carve(2 * D).rearrange("p (r h j f) -> p r h j f", r=2, h=2, j=4)
        carve = region(HN)
        M = carve(2 * 2 * 9 * HF).rearrange("p (w u m f) -> p w u m f", w=2, u=2, m=9)
        carve = region(H0)
        xg = carve(4 * 2 * 4 * HF).rearrange("p (w u j f) -> p w u j f", w=4, u=2, j=4)
        hs = carve(2 * 2 * P).rearrange("p (w n) -> p w n", w=2)
        carve = region(PART2)
        agg_t = carve(NCOMP * NP).rearrange("p (m n) -> p m n", m=NCOMP)
        xvu = carve(2 * 3 * HF).rearrange("p (u i f) -> p u i f", u=2, i=3)
        dotu = carve(2 * HF).rearrange("p (u f) -> p u f", u=2)
        carve = region(ARENA)
        agg1 = carve(NT * NCOMP * C).rearrange("p (t m f) -> p t m f", t=NT, m=NCOMP)
        s_z = carve(NP)
        s_e = carve(NP)
        s_t = carve(NP)
        v_t = carve(3 * NP).rearrange("p (i n) -> p i n", i=3)

        keyi = sb("keyi", [EP, 2, EC], I32)
        zer = sb("zer", [P, CH])
        small = sb("small", [P, 2, 4, NT])
        small_i = sb("small_i", [P, 2, NT], I32)
        start = sb("start", [P, 2, NT])
        offs = sb("offs", [P, 2, NT])
        pos = sb("pos", [EP, 2, EC], I32)
        iota_c = sb("iota_c", [P, CH])
        iota_n = sb("iota_n", [P, P])
        tilef = sb("tilef", [P, 2, CH])
        tilei = sb("tilei", [P, 2, CH], I32)
        slots0 = sb("slots0", [P, CH, W0])
        slots1 = sb("slots1", [P, CH, W1])
        slots = [slots0, slots1]
        row_st = sb("row_st", [EP, 4, W1])
        pos_st = sb("pos_st", [EP, 4, 1], I32)
        idx_st = sb("idx_st", [P, 8, 1], I32)
        local = sb("local", [P, 2, CH])
        gidx = sb("gidx", [P, 2, CH], I32)
        logit = sb("logit", [P, CH, H])
        araw = sb("araw", [P, 2, H])
        cmax = sb("cmax", [P, CH, H])
        eqt = sb("eqt", [P, NT, CH])
        nmax = sb("nmax", [P, NT, H])
        mc = sb("mc", [P, CH, H])
        mc3 = sb("mc3", [P, CH, 3, H], BF16)
        O = sb("O", [P, 4, P])
        pen = sb("pen", [P, 2, P])
        OTf = sb("OTf", [P, 2, P])
        ident = sb("ident", [P, P])
        ones = sb("ones", [P, P])
        tri = sb("tri", [P, P])
        stats = sb("stats", [P, NT, 6])
        mv = sb("mv", [P, NT, 2])
        std = sb("std", [P, NT])
        rstd = sb("rstd", [P, NT])
        eps = sb("eps", [P, 1])
        lnp = sb("lnp", [P, 4, KT])
        b1col = sb("b1col", [P, FT])
        brow = sb("brow", [P, 3 * D])
        den = sb("den", [P, 2, NT * H])
        wf1 = sb("wf1", [NRBF, C])
        bf1 = sb("bf1", [C, 1])
        wf2 = sb("wf2", [P, 2, 4 * HF])
        bf2 = sb("bf2", [1, 2, 4 * HF])
        wfr = mc[:, :, :].rearrange("p c h -> p (c h)")[:, 0:4 * C]
        zero_w = sb("zero_w", [P, 512])
        win = sb("win", [P, 2, C])
        w1sv = sb("w1sv", [P, 2, 2, C])
        w2sv = sb("w2sv", [P, 2, C])
        bfraw = cmax[0:1, :, :].rearrange("p c h -> p (c h)")[:, 0:4 * C]

        PS = ctx.enter_context(nc.psum_tensor("PS", [P, 8, 512], F32))

        def pair(b):
            return PS[:, b:b + 2, :].rearrange("p b n -> p (b n)")

        def XB(t):
            return (4, 5, 6, 7, 2)[t]

        def OB(t):
            return (2, 3, 4, 5, 6)[t]

        sems = {}

        def S(name):
            if name not in sems:
                sems[name] = ctx.enter_context(nc.semaphore(name))
            return sems[name]

        class Chain:

            def __init__(self, eng, name):
                self.eng, self.sem, self.n = eng, S(name), 0

            def __call__(self, ins):
                self.n += 1
                ins.then_inc(self.sem, 1)
                self.eng.wait_ge(self.sem, self.n)

        class LoopChain:

            def __init__(self, eng, name, per):
                self.eng, self.sem, self.per, self.n, self.base = eng, S(name), per, 0, 0

            def turn(self, i):
                self.i, self.n = i, 0

            def __call__(self, ins):
                self.n += 1
                ins.then_inc(self.sem, 1)
                self.eng.wait_ge(self.sem, self.base + self.i * self.per + self.n)

            def mark(self, ins):
                self.n += 1
                ins.then_inc(self.sem, 1)
                return self.base + self.i * self.per + self.n

        def quads(eng, body):
            for v in range(4):
                body(v, v, 0)
            with eng.Fori(1, QUADS - 1) as i:
                for v in range(4):
                    body(i * 4 + v, v, i)
            for v in range(4):
                body(CH - 4 + v, v, QUADS - 1)

        def within(c, back=0, ahead=0):
            return not isinstance(c, int) or (c - back >= 0 and c + ahead < CH)

        block = ctx.enter_context(nc.Block())

        @block.sync
        def _(sp):
            sp.dma_start(keyi[:, 0, :], A["dst"].rearrange("(p c) -> p c", p=EP)).then_inc(S("ld_keys"), 16)
            sp.dma_start(keyi[:, 1, :], A["src"].rearrange("(p c) -> p c", p=EP)).then_inc(S("ld_keys"), 16)
            for t in range(NT):
                if ROWS[t] == P:
                    continue
                sp.wait_ge(S("x_pad"), 1)
            for t in range(NT):
                sp.dma_start(X[0:ROWS[t], t, :], A["x"][P * t:P * t + ROWS[t], :]).then_inc(S("ld_x"), 16)
            for a, name in enumerate(("edge_attr_8", "edge_attr_8_n2")):
                sp.dma_start(raw0[:, a, :, :],
                             A[name].rearrange("(p c) h -> p c h", p=EP)).then_inc(S("ld_bias"), 16)
            sp.dma_start(raw_r, A["edge_attr_3"].rearrange("(p c) i -> p c i", p=EP)).then_inc(S("ld_r"), 16)
            sp.dma_start(rnorm[:, 1, :], A["edge_weight"].rearrange("(p c) -> p c", p=EP)).then_inc(S("ld_r"), 16)
            sp.dma_start(pack[1][:, :, 6:W1], A["edge_attr_20"].rearrange("(p c) f -> p c f", p=EP)).then_inc(S("ld_f"), 16)
            sp.dma_start(wqkv, A["L0_gnn_Wqkv"].rearrange("(k p) n -> p k n", p=P)).then_inc(S("ld_wqkv"), 16)
            sp.dma_start(brow[:, :], A["L0_gnn_bqkv"].rearrange("(a n) -> a n", a=1).to_broadcast([P, 3 * D])).then_inc(S("ld_brow"), 16)
            for k in range(2):
                sp.wait_ge(S("dummy"), k + 1)
                w = (W0, W1)[k]
                sp.dma_start(slots_dram[k][:, :].rearrange("(p c) w -> p c w", p=P),
                             slots[k][:, :, :]).then_inc(S(f"filled{k}"), 16)
            for t in range(NT):
                sp.wait_ge(S("qv_rows"), t + 1)
                r = ROWS[t]
                sp.dma_start(q_table[P * t:P * t + r, :], qst[0:r, t % 2, 0, :]).then_inc(S(f"st_qv{t % 2}"), 16)
                sp.dma_start(v_table[P * t:P * t + r, :], qst[0:r, t % 2, 1, :]).then_inc(S(f"st_qv{t % 2}"), 16)
            def reload(k):
                for v in range(4):
                    sp.wait_ge(S(f"scattered{k}_{v}"), 16 * (EC // 4))
                sp.dma_start(slots[k][:, :, :],
                             slots_dram[k][:, :].rearrange("(c p) w -> p c w", p=P)).then_inc(S(f"ld_slots{k}"), 16)

            reload(0)
            sp.wait_ge(S("qkv_mm"), 3 * NT)
            sp.dma_start(w1, A["L0_gnn_W1"].rearrange("(k p) n -> p k n", p=P)).then_inc(S("ld_w1"), 16)
            sp.wait_ge(S("qkv_sb"), 3 * NT)
            for j, name in enumerate(("L0_gnn_bo", "L0_gnn_b2")):
                sp.dma_start(brow[:, j * D:(j + 1) * D], A[name].rearrange("(a n) -> a n", a=1).to_broadcast([P, D])
                             ).then_inc(S("ld_b2rows"), 16)
            sp.wait_ge(S("shifted"), 1)
            sp.dma_start(wfr, A["L1_gnn_Wf2"][:, 0:4 * C]).then_inc(S("ld_wf2"), 16)
            sp.dma_start(bfraw, A["L1_gnn_bf2"][0:4 * C].rearrange("(a n) -> a n", a=1)).then_inc(S("ld_wf2"), 16)
            sp.wait_ge(S("mx_mm"), CH)
            w2_dram = A["L0_gnn_W2"].rearrange("(f p) n -> p f n", p=P)
            sp.dma_start(w2[:, 0:W2_EARLY, :], w2_dram[:, 0:W2_EARLY, :]).then_inc(S("ld_w2a"), 16)
            reload(1)
            sp.dma_start(w2[:, W2_EARLY:, :], w2_dram[:, W2_EARLY:, :]).then_inc(S("ld_w2b"), 16)
            for t in range(NT):
                sp.wait_ge(S("x_rows"), t + 1)
                r = ROWS[t]
                for h in range(2):
                    sp.dma_start(x_table[h][P * t:P * t + r, :],
                                 xst[0:r, t % 2, h, :, :].rearrange("p j f -> p (j f)")).then_inc(S(f"st_x{t % 2}"), 16)
            for t in range(NT):
                sp.wait_ge(S("out_rows"), t + 1)
                sp.dma_start(out[P * t:P * t + ROWS[t], :], X[0:ROWS[t], t, :]).then_inc(S("st_out"), 16)
            sp.wait_ge(S("st_out"), 16 * NT)

        @block.gpsimd
        def _(pool):
            link = Chain(pool, "pool_chain")
            pool.memset(X[:, NT - 1, :], 0.0).then_inc(S("x_pad"), 1)
            pool.memset(zer[:, :], 0.0).then_inc(S("consts"), 1)
            pool.memset(zero_w[:, :], 0.0)
            pool.memset(eps[:, :], EPS).then_inc(S("consts"), 1)
            pool.memset(ones[:, :], 1.0).then_inc(S("consts"), 1)
            link(pool.memset(ident[:, :], 0.0))
            pool.affine_select(out=ident[:, :], in_=ident[:, :], compare_op=ALU.not_equal, fill=1.0, base=0,
                               pattern=[[-1, P]], channel_multiplier=1).then_inc(S("consts"), 1)
            link(pool.memset(tri[:, :], 1.0))
            pool.affine_select(out=tri[:, :], in_=tri[:, :], compare_op=ALU.is_gt, fill=0.0, base=0,
                               pattern=[[1, P]], channel_multiplier=-1).then_inc(S("consts"), 1)
            pool.iota(iota_n[:, :], pattern=[[1, P]], base=0, channel_multiplier=0,
                      allow_small_or_imprecise_dtypes=True).then_inc(S("consts"), 1)
            pool.iota(iota_c[:, :], pattern=[[1, CH]], base=0, channel_multiplier=0,
                      allow_small_or_imprecise_dtypes=True).then_inc(S("consts"), 1)
            link(pool.memset(slots0[:, :, :], 0.0))
            pool.memset(slots0[:, :, 0:1], -1.0).then_inc(S("dummy"), 1)
            link(pool.memset(slots1[:, :, :], 0.0))
            pool.memset(slots1[:, :, 0:1], -1.0).then_inc(S("dummy"), 1)

            def scatter_edges(k, w):
                pool.wait_ge(S("packed"), k + 1)
                pool.wait_ge(S(f"filled{k}"), 16)

                def one(i, v):
                    pool.tensor_copy(out=row_st[:, v, 0:w],
                                     in_=pack[k][:, ds(i * 4 + v, 1), :].rearrange("p a w -> p (a w)")
                                     ).then_inc(S(f"staged{k}"), 1)
                    pool.tensor_copy(out=pos_st[:, v, :], in_=pos[:, k, ds(i * 4 + v, 1)]).then_inc(S(f"staged{k}"), 1)
                    pool.wait_ge(S(f"staged{k}"), i * 8 + 2 * v + 2)
                    pool.sem_inc(S(f"scatter_go{k}"), 1)
                    pool.indirect_dma_start(
                        out=slots_dram[k][:, :], out_offset=bass.IndirectOffsetOnAxis(ap=pos_st[:, v, :], axis=0),
                        in_=row_st[:, v, 0:w], in_offset=None).then_inc(S(f"scattered{k}_{v}"), 16)

                for v in range(4):
                    one(0, v)
                with pool.Fori(1, EC // 4) as i:
                    for v in range(4):
                        pool.wait_ge(S(f"scattered{k}_{v}"), i * 16)
                        one(i, v)

            def gather(dst, table, layer, c, v, count, landed):
                pool.tensor_copy(out=idx_st[:, v, :], in_=gidx[:, layer, ds(c, 1)]).then_inc(S(count), 1)
                pool.wait_ge(S(count), c + 1)
                pool.sem_inc(S("gather_go"), 1)
                pool.indirect_dma_start(out=dst, out_offset=None, in_=table[:, :],
                                        in_offset=bass.IndirectOffsetOnAxis(ap=idx_st[:, v, :], axis=0)
                                        ).then_inc(S(landed), 16)

            scatter_edges(0, W0)

            def first_pass(c, v, i):
                a = (v + 3) % 4
                if within(c, ahead=3):
                    if within(c, back=1):
                        pool.wait_ge(S("prod_done"), c + 2)
                    gather(qg[:, a, :], q_table, 0, c + 3, a, "idx0", f"q_in{a}")
                u = v % 2
                pool.wait_ge(S("logit_done"), c + 1)
                if within(c, back=2):
                    pool.wait_ge(S("mask_t"), c + 1)
                pool.tensor_tensor(
                    out=masked[:, u, 0:H // 2, :],
                    in0=pen[:, u, :].unsqueeze(1).to_broadcast([P, H // 2, P]),
                    in1=logit[:, ds(c, 1), 0:H // 2].rearrange("p a h -> p (a h)").unsqueeze(2).to_broadcast([P, H // 2, P]),
                    op=ALU.add).then_inc(S("mask_done"), 1)

            pool.wait_ge(S("slots_ready"), 1)
            for u in range(2):
                pool.wait_ge(S(f"st_qv{u}"), 32 * len(range(u, NT, 2)))
            for c in range(3):
                gather(qg[:, c, :], q_table, 0, c, c, "idx0", f"q_in{c}")
            quads(pool, first_pass)

            def second_pass(c, v, i):
                if within(c, back=4):
                    pool.wait_ge(S("msg_done"), c - 1)
                gather(qg[:, v, :], v_table, 0, c, v, "idx1", f"v_in{v}")

            pool.wait_ge(S("prod_done"), CH + 2)
            quads(pool, second_pass)

            scatter_edges(1, W1)

            pool.wait_ge(S("slots_ready"), 2)
            pool.wait_ge(S("h_done"), CH // G4)
            for u in range(2):
                pool.wait_ge(S(f"st_x{u}"), 32 * len(range(u, NT, 2)))
            for half in range(2):
                def gather_pair(pr, w, first):
                    c = (pr - half * 2 * QUADS) * 2
                    if not first:
                        pool.wait_ge(S("m_done"), pr - 1)
                    pool.tensor_copy(out=idx_st[:, 2 * w:2 * w + 2, 0], in_=gidx[:, 1, ds(c, 2)]).then_inc(S("idx2"), 1)
                    pool.wait_ge(S("idx2"), pr + 1)
                    pool.sem_inc(S("gather_go"), 1)
                    for u in range(2):
                        pool.indirect_dma_start(
                            out=xg[:, w, u, :, :].rearrange("p j f -> p (j f)"), out_offset=None,
                            in_=x_table[half][:, :],
                            in_offset=bass.IndirectOffsetOnAxis(ap=idx_st[:, 2 * w + u, :], axis=0)
                        ).then_inc(S(f"x_in{w}"), 16)

                base = half * 2 * QUADS
                for n in range(4):
                    gather_pair(base + n, (base + n) % 4, half == 0)
                with pool.Fori(1, 2 * QUADS // 4) as i:
                    for n in range(4):
                        gather_pair(i * 4 + n + base, (base + n) % 4, False)
                for n in range(2 * QUADS // 4 * 4, 2 * QUADS):
                    gather_pair(base + n, (base + n) % 4, False)

        @block.scalar
        def _(act):
            link = Chain(act, "act_chain")
            for i, name in enumerate(("L0_gnn_ln1_g", "L0_gnn_ln1_b", "L0_gnn_ln2_g", "L0_gnn_ln2_b")):
                act.dma_start(lnp[:, i, :], A[name].rearrange("(k p) -> p k", p=P), allow_slow_non_contiguous=True).then_inc(S("ld_small"), 16)
            act.dma_start(b1col[:, :], A["L0_gnn_b1"].rearrange("(k p) -> p k", p=P), allow_slow_non_contiguous=True).then_inc(S("ld_small"), 16)
            act.dma_start(WO[:, :, :], A["L0_gnn_Wo"].rearrange("(k p) n -> p k n", p=P)).then_inc(S("ld_wo"), 16)
            small_loads = [
                (wf1[:, :], A["L1_gnn_Wf1"]), (bf1[:, :], A["L1_gnn_bf1"].rearrange("(p a) -> p a", a=1)),
                (win[:, 0, :], A["L1_gnn_W_in2f_s"]), (win[:, 1, :], A["L1_gnn_W_in2f_v"]),
                (w1sv[:, 0, :, :], A["L1_gnn_W1_s"].rearrange("(f a) c -> f a c", a=2)),
                (w1sv[:, 1, :, :], A["L1_gnn_W1_v"].rearrange("(f a) c -> f a c", a=2)),
                (w2sv[:, 0, :], A["L1_gnn_W2_s"]), (w2sv[:, 1, :], A["L1_gnn_W2_v"]),
            ]
            for dst, src in small_loads:
                act.dma_start(dst, src).then_inc(S("ld_l1"), 16)

            def sqrt_var(k):
                act.wait_ge(S("ln_stats"), k)
                act.wait_ge(S("consts"), 7)
                act.activation(std[:, :], mv[:, :, 1], ACT.Sqrt, bias=eps[:, :]).then_inc(S("ln_std"), 1)

            def evac_ht(g, first, done, total, scale_bias):
                for k in range(g):
                    act.wait_ge(S(first), k + 1)
                    kw = scale_bias(k)
                    act.activation(ht[:, k, :], pair(2 * (k % 2))[:, 0:NP], ACT.Identity, **kw).then_inc(S(done), 1)

            act.wait_ge(S("rsq_done"), 1)
            act.activation(rnorm[:, 0, :], rnorm[:, 0, :], ACT.Sqrt).then_inc(S("rnorm_done"), 1)
            sqrt_var(1)
            sqrt_var(2)
            act.wait_ge(S("ld_small"), 80)
            evac_ht(KT, "t1_ps", "ht1", KT, lambda k: dict(scale=lnp[:, 0, k:k + 1], bias=lnp[:, 1, k:k + 1]))

            def transposed_one_hot(c, u):
                act.wait_ge(S("ot_ps"), c + 3)
                if within(c, back=2):
                    act.wait_ge(S("kg_mm"), c + 1)
                act.activation(OTf[:, u, :], PS[:, 7, 0:P], ACT.Copy).then_inc(S("ot_f"), 1)
                act.activation(OTb[:, ds(c * P, P)], PS[:, 7, 0:P], ACT.Copy).then_inc(S("ot_b"), 1)

            def first_pass(c, v, i):
                if within(c, ahead=1):
                    transposed_one_hot(c + 1, (v + 1) % 2)
                u = v % 2
                act.wait_ge(S("logit_done"), c + 1)
                if within(c, back=2):
                    act.wait_ge(S("mask_t"), c + 1)
                for h in range(H // 2, H):
                    ins = act.activation(masked[:, u, h, :], pen[:, u, :], ACT.Identity, bias=logit[:, ds(c, 1), h])
                ins.then_inc(S("mask_done_a"), 1)

            transposed_one_hot(0, 0)
            quads(act, first_pass)

            act.wait_ge(S("shifted"), 1)
            act.activation(logit[:, :, :], logit[:, :, :], ACT.Exp).then_inc(S("exp_done"), 1)

            for k in range(KT):
                act.wait_ge(S("t2_ps"), k + 1)
                act.activation(ht[:, k, :], pair(6)[:, 0:NP] if k % 2 else pair(4)[:, 0:NP], ACT.Copy).then_inc(S("ht2"), 1)
            sqrt_var(3)
            act.wait_ge(S("wo_mm"), NT)
            evac_ht(KT, "t3_ps", "ht3", KT, lambda k: dict(scale=lnp[:, 2, k:k + 1], bias=lnp[:, 3, k:k + 1]))
            for f in range(FT):
                act.wait_ge(S("w1_mm"), f + 1)
                act.activation(gelu_t[:, f, :].rearrange("p (a n) -> p a n", a=2),
                               PS[:, 4 + 2 * (f % 2):6 + 2 * (f % 2), 0:NH], ACT.Gelu,
                               bias=b1col[:, f:f + 1]).then_inc(S("gelu"), 1)
            act.wait_ge(S("ld_l1"), 16 * len(small_loads))
            for g in range(CH // G4):
                r = g % 2
                act.wait_ge(S("z_mm"), g + 1)
                if g >= 2:
                    act.wait_ge(S("zrelu"), g - 1)
                act.activation(zed[:, r, :], PS[:, 6 + r, :], ACT.Identity, bias=bf1[:, :]).then_inc(S("z_sb"), 1)
                act.wait_ge(S("znab"), g + 1)
                if g >= 2:
                    act.wait_ge(S("h_done"), g - 1)
                act.activation(zln[:, r, :], znab[:, :], ACT.Exp).then_inc(S("z_exp"), 1)
                act.wait_ge(S("z_exp"), g + 1)
                act.activation(zln[:, r, :], zln[:, r, :], ACT.Ln, bias=1.0).then_inc(S("z_ln"), 1)

            sqrt_var(4)
            for j in range(4):
                act.wait_ge(S("t4_ps"), j + 1)
                act.activation(xin_t[:, j, :], pair(2 * (j % 2))[:, 0:NP], ACT.Copy).then_inc(S("ht4"), 1)

            for half in range(2):
                with act.Fori(0, QUADS) as i:
                    for w in range(2):
                        pr = i * 2 + w + half * 2 * QUADS
                        act.wait_ge(S("w_mm"), pr + 1)
                        act.activation(hs[:, w, :], h_t[:, ds((i * 4 + 2 * w) * P, 2 * P)], ACT.Copy
                                       ).then_inc(S("hs_done"), 1)

            for m in range(NCOMP):
                act.wait_ge(S("t5_ps"), m + 1)
                act.activation(agg_t[:, m, :], pair(2 * (m % 2))[:, 0:NP], ACT.Copy, scale=COMP_SCALE[m]
                               ).then_inc(S("at_sb"), 1)
            act.wait_ge(S("s_mm"), 1)
            act.activation(s_z.rearrange("p (a n) -> p a n", a=2), PS[:, 4:6, 0:NH], ACT.Copy).then_inc(S("sz"), 1)
            act.wait_ge(S("s_abs"), 1)
            link(act.activation(s_t[:, :], s_e[:, :], ACT.Exp))
            act.activation(s_e[:, :], s_t[:, :], ACT.Ln, bias=1.0).then_inc(S("s_ln"), 1)
            for i in range(3):
                act.wait_ge(S("v_mm"), i + 1)
                act.activation(v_t[:, i, :].rearrange("p (a n) -> p a n", a=2),
                               PS[:, 6:8, 0:NH] if i % 2 == 0 else PS[:, 0:2, 0:NH], ACT.Copy).then_inc(S("v_sb"), 1)

        @block.vector
        def _(dve):
            link = Chain(dve, "dve_chain")
            for name in ("prod_done", "mask_t", "kg_mm", "max_done", "mask_done", "msg_done", "agg_mm",
                         "m_done", "w_mm", "agg1_mm", "ot_ps", "mask_done_a"):
                dve.sem_inc(S(name), 2)
            dve.sem_inc(S("ot_b"), 1)

            dve.wait_ge(S("consts"), 7)
            dve.wait_ge(S("ld_keys"), 32)

            def bucket(k):
                link(dve.tensor_copy(out=keyf[:, k, :], in_=keyi[:, k, :]))
                dve.memset(ge[:, 0, :], 1.0)
                link(dve.memset(ge[:, NT, :], 0.0))
                for t in range(1, NT):
                    ins = dve.tensor_scalar(ge[:, t, :], keyf[:, k, :], float(P * t), None, ALU.is_ge)
                    link(ins)
                link(dve.tensor_tensor(out=in_b, in0=ge[:, 0:NT, :], in1=ge[:, 1:NT + 1, :], op=ALU.subtract))
                for t in range(NT):
                    link(dve.tensor_tensor_scan(out=cum[:, t, :], data0=in_b[:, t, :], data1=zer[0:EP, 0:EC],
                                                initial=0.0, op0=ALU.add, op1=ALU.add))
                dve.sem_inc(S("counts"), 1)
                dve.wait_ge(S("prefix"), k + 1)
                link(dve.tensor_copy(out=small[:, k, 0:2, :], in_=PS[:, 0, 0:2 * NT].rearrange("p (a t) -> p a t", a=2)))
                link(dve.tensor_scalar(small[:, k, 2, :], small[:, k, 1, :], float(P - 1), None, ALU.add))
                link(dve.tensor_copy(out=small_i[:, k, :], in_=small[:, k, 2, :]))
                link(dve.tensor_scalar(small_i[:, k, :], small_i[:, k, :], 7, None, ALU.arith_shift_right))
                link(dve.tensor_copy(out=small[:, k, 3, :], in_=small_i[:, k, :]))
                link(dve.memset(start[:, k, 0:1], 0.0))
                link(dve.tensor_tensor_scan(out=start[:, k, 1:NT], data0=small[:, k, 3, 0:NT - 1],
                                            data1=zer[:, 0:NT - 1], initial=0.0, op0=ALU.add, op1=ALU.add))
                link(dve.scalar_tensor_tensor(out=offs[:, k, :], in0=start[:, k, :], scalar=float(P),
                                              in1=small[:, k, 0, :], op0=ALU.mult, op1=ALU.add))
                link(dve.tensor_scalar(offs[:, k, :], offs[:, k, :], -1.0, None, ALU.add))
                for t in range(NT):
                    link(dve.scalar_tensor_tensor(out=cum[:, t, :], in0=cum[:, t, :], scalar=offs[0:EP, k, t:t + 1],
                                                  in1=in_b[:, t, :], op0=ALU.add, op1=ALU.mult))
                for t in range(1, NT):
                    link(dve.tensor_tensor(out=cum[:, 0, :], in0=cum[:, 0, :], in1=cum[:, t, :], op=ALU.add))
                link(dve.tensor_copy(out=pos[:, k, :], in_=cum[:, 0, :]))
                link(dve.tensor_scalar(tilef[:, k, :], iota_c[:, :], start[:, k, 1:2], None, ALU.is_ge))
                for t in range(2, NT):
                    link(dve.scalar_tensor_tensor(out=tilef[:, k, :], in0=iota_c[:, :], scalar=start[:, k, t:t + 1],
                                                  in1=tilef[:, k, :], op0=ALU.is_ge, op1=ALU.add))
                dve.tensor_copy(out=tilei[:, k, :], in_=tilef[:, k, :]).then_inc(S("tiles"), 1)
                link(dve.tensor_copy(out=pack[k][:, :, 0], in_=keyf[:, k, :]))
                link(dve.tensor_copy(out=pack[k].bitcast(I32)[:, :, 1], in_=keyi[:, 1 - k, :]))

            dve.wait_ge(S("ld_r"), 32)
            link(dve.tensor_tensor(out=rsq, in0=raw_r, in1=raw_r, op=ALU.mult))
            link(dve.tensor_reduce(out=rnorm[:, 0, :], in_=rsq, axis=X_AXIS, op=ALU.add))
            dve.sem_inc(S("rsq_done"), 1)
            bucket(0)
            dve.wait_ge(S("ld_bias"), 32)
            link(dve.tensor_tensor(out=pack[0][:, :, 2:W0], in0=raw0[:, 0, :, :], in1=raw0[:, 1, :, :], op=ALU.add))
            dve.sem_inc(S("packed"), 1)

            def row_stats(src):
                for t in range(NT):
                    link(dve.bn_stats(stats[:, t, :], src[:, t, :]))
                    ins = dve.bn_aggr(mv[:, t, :], stats[:, t, :])
                    if t < NT - 1:
                        link(ins)
                ins.then_inc(S("ln_stats"), 1)

            def normalise(k, src, dst, done=None):
                dve.wait_ge(S("ln_std"), k)
                link(dve.reciprocal(rstd[:, :], std[:, :]))
                for t in range(NT):
                    ins = dve.tensor_scalar(dst[:, t, :], src[:, t, :], mv[:, t, 0:1], rstd[:, t:t + 1],
                                            ALU.subtract, ALU.mult)
                    if done:
                        ins.then_inc(S(done), 1)
                    else:
                        link(ins)

            dve.wait_ge(S("ld_x"), 16 * NT)
            row_stats(X)
            normalise(1, X, h0)
            link(dve.tensor_scalar(H0[:, :], H0[:, :], 0.0, None, ALU.max))
            row_stats(h0)
            normalise(2, h0, hn, "hn1")

            bucket(1)
            dve.wait_ge(S("ld_f"), 16)
            dve.wait_ge(S("rnorm_done"), 1)
            link(dve.reciprocal(rnorm[:, 0, :], rnorm[:, 0, :]))
            link(dve.tensor_tensor(out=pack[1][:, :, 3:6], in0=raw_r,
                                   in1=rnorm[:, 0, :].unsqueeze(2).to_broadcast([EP, EC, 3]), op=ALU.mult))
            link(dve.tensor_copy(out=pack[1][:, :, 2], in_=rnorm[:, 1, :]))
            dve.sem_inc(S("packed"), 1)

            dve.wait_ge(S("ld_brow"), 16)
            for t in range(NT):
                for j in range(3):
                    n = 3 * t + j
                    dve.wait_ge(S("qkv_mm"), n + 1)
                    if t >= 2 and j == 0:
                        dve.wait_ge(S(f"st_qv{t % 2}"), 32 * (t // 2))
                    dst = (qst[:, t % 2, 0, :], K_sb[:, t, :], qst[:, t % 2, 1, :])[j]
                    ins = dve.tensor_tensor(out=dst, in0=PS[:, 4 + n % 4, :], in1=brow[:, j * D:(j + 1) * D], op=ALU.add)
                    ins.then_inc(S("qkv_sb"), 1)
                dve.wait_ge(S("qkv_sb"), 3 * t + 3)
                dve.sem_inc(S("qv_rows"), 1)

            def slot_data(k):
                dve.wait_ge(S(f"ld_slots{k}"), 16)
                link(dve.scalar_tensor_tensor(out=local[:, k, :], in0=tilef[:, k, :], scalar=float(-P),
                                              in1=slots[k][:, :, 0], op0=ALU.mult, op1=ALU.add))
                link(dve.tensor_copy(out=gidx[:, k, :], in_=slots[k][:, :, :].bitcast(I32)[:, :, 1]))
                dve.sem_inc(S("slots_ready"), 1)

            slot_data(0)

            def onehot(c, u):
                if within(c, back=2):
                    dve.wait_ge(S("ot_ps"), c + 1)
                dve.tensor_scalar(O[:, u, :], iota_n[:, :], local[:, 0, ds(c, 1)], None, ALU.is_equal).then_inc(S("oh_done"), 1)
                if within(c, back=2):
                    dve.wait_ge(S("mask_done"), c + 1)
                    dve.wait_ge(S("mask_done_a"), c + 1)
                dve.tensor_scalar(pen[:, u, :], iota_n[:, :], local[:, 0, ds(c, 1)], -PENALTY, ALU.not_equal, ALU.mult
                                  ).then_inc(S("pen_done"), 1)

            def logits(c, v, turn):
                u = v % 2
                dve.wait_ge(S(f"q_in{v}"), turn * 16 + 16)
                dve.wait_ge(S("kg_mm"), c + 3)
                dve.tensor_tensor(out=msg[:, u, :], in0=PS[:, 4 + u, :], in1=qg[:, v, :], op=ALU.mult
                                  ).then_inc(S("prod_done"), 1)
                dve.wait_ge(S("prod_done"), c + 3)
                dve.tensor_reduce(out=araw[:, u, :], in_=msg[:, u, :].rearrange("p (h d) -> p h d", h=H),
                                  axis=X_AXIS, op=ALU.add).then_inc(S("red_done"), 1)
                dve.wait_ge(S("red_done"), c + 1)
                dve.scalar_tensor_tensor(out=logit[:, ds(c, 1), :].rearrange("p a h -> p (a h)"), in0=araw[:, u, :],
                                         scalar=float(D) ** -0.5,
                                         in1=slots0[:, ds(c, 1), 2:W0].rearrange("p a h -> p (a h)"),
                                         op0=ALU.mult, op1=ALU.add).then_inc(S("logit_done"), 1)

            def chunk_max(c, u):
                dve.wait_ge(S("mask_t"), c + 3)
                dve.tensor_reduce(out=cmax[:, ds(c, 1), :].rearrange("p a h -> p (a h)"),
                                  in_=pair(2 * u).rearrange("p (h n) -> p h n", h=H),
                                  axis=X_AXIS, op=ALU.max).then_inc(S("max_done"), 1)

            def first_pass(c, v, i):
                if within(c, ahead=1):
                    onehot(c + 1, (v + 1) % 2)
                logits(c, v, i)
                if within(c, back=2):
                    chunk_max(c - 2, v % 2)

            onehot(0, 0)
            quads(dve, first_pass)
            chunk_max(CH - 2, 0)
            chunk_max(CH - 1, 1)
            dve.wait_ge(S("max_done"), CH + 2)

            for t in range(NT):
                link(dve.tensor_scalar(eqt[:, t, :], tilef[:, 0, :], float(t), None, ALU.is_equal))
            for t in range(NT):
                link(dve.tensor_scalar(zer[:, :], eqt[:, t, :], 1.0, PENALTY, ALU.subtract, ALU.mult))
                link(dve.tensor_tensor(out=mc[:, :, :], in0=cmax[:, :, :],
                                       in1=zer[:, :].unsqueeze(2).to_broadcast([P, CH, H]), op=ALU.add))
                link(dve.tensor_reduce(out=nmax[:, t, :], in_=mc[:, :, :].rearrange("p c h -> p h c"),
                                       axis=X_AXIS, op=ALU.max))
            for t in range(NT):
                dst = cmax if t else mc
                link(dve.tensor_tensor(out=dst[:, :, :], in0=nmax[:, t, :].unsqueeze(1).to_broadcast([P, CH, H]),
                                       in1=eqt[:, t, :].unsqueeze(2).to_broadcast([P, CH, H]), op=ALU.mult))
                if t:
                    link(dve.tensor_tensor(out=mc[:, :, :], in0=mc[:, :, :], in1=cmax[:, :, :], op=ALU.add))
            for part in range(3):
                link(dve.tensor_copy(out=mc3[:, :, part, :], in_=mc[:, :, :]))
                if part < 2:
                    link(dve.tensor_tensor(out=mc[:, :, :], in0=mc[:, :, :], in1=mc3[:, :, part, :], op=ALU.subtract))
            dve.sem_inc(S("mc_done"), 1)
            for b in range(CH // QB):
                dve.wait_ge(S("mx_mm"), QB * (b + 1))
                for part in range(3):
                    lg = logit[:, QB * b:QB * (b + 1), :]
                    mx = PS[:, b, 0:QB * 3 * H].rearrange("p (c a h) -> p c a h", a=3, h=H)[:, :, part, :]
                    link(dve.tensor_tensor(out=lg, in0=lg, in1=mx, op=ALU.subtract))
            dve.sem_inc(S("shifted"), 1)
            dve.wait_ge(S("exp_done"), 1)

            def second_pass(c, v, i):
                u = v % 2
                if within(c, back=2):
                    dve.wait_ge(S("agg_mm"), c + 1)
                dve.tensor_scalar(O[:, u, :], iota_n[:, :], local[:, 0, ds(c, 1)], None, ALU.is_equal
                                  ).then_inc(S("oh2_done"), 1)
                dve.wait_ge(S(f"v_in{v}"), i * 16 + 16)
                dve.tensor_tensor(out=msg[:, u, :].rearrange("p (h d) -> p h d", h=H),
                                  in0=qg[:, v, :].rearrange("p (h d) -> p h d", h=H),
                                  in1=logit[:, ds(c, 1), :].rearrange("p a h -> p (a h)").unsqueeze(2).to_broadcast([P, H, DH]),
                                  op=ALU.mult).then_inc(S("msg_done"), 1)

            quads(dve, second_pass)

            dve.wait_ge(S("agg_closed"), 1)
            link(dve.tensor_copy(out=den[:, 0, :], in_=PS[:, 5, 0:NT * H]))
            link(dve.scalar_tensor_tensor(out=den[:, 1, :], in0=den[:, 0, :], scalar=0.0, in1=den[:, 0, :],
                                          op0=ALU.is_equal, op1=ALU.add))
            link(dve.reciprocal(den[:, 0, :], den[:, 1, :]))
            for t in range(NT):
                dve.tensor_tensor(out=hn[:, t, :].rearrange("p (h d) -> p h d", h=H),
                                  in0=PS[:, t, :].rearrange("p (h d) -> p h d", h=H),
                                  in1=den[:, 0, t * H:(t + 1) * H].unsqueeze(2).to_broadcast([P, H, DH]),
                                  op=ALU.mult).then_inc(S("att_sb"), 1)
            dve.wait_ge(S("ld_b2rows"), 32)
            for t in range(NT):
                link(dve.tensor_tensor(out=h0[:, t, :], in0=h0[:, t, :], in1=brow[:, 0:D], op=ALU.add))
            for t in range(NT):
                dve.wait_ge(S("wo_mm"), t + 1)
                link(dve.tensor_tensor(out=h0[:, t, :], in0=PS[:, t % 4, :], in1=h0[:, t, :], op=ALU.add))
                dve.sem_inc(S("h1_sb"), 1)
            row_stats(h0)
            dve.wait_ge(S("t2_ps"), KT)
            normalise(3, h0, hn, "hn3")
            for t in range(NT):
                link(dve.tensor_tensor(out=h0[:, t, :], in0=h0[:, t, :], in1=brow[:, D:2 * D], op=ALU.add))
                link(dve.tensor_tensor(out=X[:, t, :], in0=h0[:, t, :], in1=X[:, t, :], op=ALU.add))
            dve.wait_ge(S("ld_wf2"), 32)
            for h in range(2):
                for b, at in enumerate((2 * C, 0, 1, 2 * C + 1)):
                    at += 2 * HF * h
                    for dst, src in ((wf2, wfr), (bf2, bfraw)):
                        link(dve.tensor_copy(out=dst[:, h, b * HF:(b + 1) * HF], in_=src[:, at:at + 2 * HF - 1:2]))
            slot_data(1)
            dve.wait_ge(S("t3_ps"), KT)
            dve.wait_ge(S("w1_mm"), FT)
            def tiles_out(upto):
                while x1_tiles[0] < upto:
                    t = x1_tiles[0]
                    dve.wait_ge(S("w2_mm"), t + 1)
                    link(dve.tensor_tensor(out=X[:, t, :], in0=PS[:, t % 4, :], in1=X[:, t, :], op=ALU.add))
                    dve.sem_inc(S("x1_sb"), 1)
                    x1_tiles[0] += 1

            x1_tiles = [0]
            for g in range(CH // G4):
                r = g % 2
                tiles_out((g - 1) // 4)
                dve.wait_ge(S("ft_t"), g + 1)
                if g >= 2:
                    dve.wait_ge(S("z_mm"), g - 1)
                dve.tensor_copy(out=ft[0:NRBF, r, :], in_=PS[0:NRBF, 4 + r, :]).then_inc(S("ft_sb"), 1)
                dve.wait_ge(S("z_sb"), g + 1)
                if g:
                    dve.wait_ge(S("z_exp"), g)
                dve.scalar_tensor_tensor(out=znab[:, :], in0=zed[:, r, :], scalar=-1.0, in1=zed[:, r, :],
                                         op0=ALU.mult, op1=ALU.min).then_inc(S("znab"), 1)
                dve.tensor_scalar(zrelu[:, r, :], zed[:, r, :], 0.0, -LOG2, ALU.max, ALU.add).then_inc(S("zrelu"), 1)
                dve.wait_ge(S("zrelu"), g + 1)
                dve.wait_ge(S("z_ln"), g + 1)
                dve.tensor_tensor(out=h_t[:, g * G4 * P:(g + 1) * G4 * P], in0=zln[:, r, :], in1=zrelu[:, r, :], op=ALU.add
                                  ).then_inc(S("h_done"), 1)
            tiles_out(NT)

            row_stats(X)
            dve.wait_ge(S("t3_ps"), KT)
            normalise(4, X, hn)
            for t in range(NT):
                dve.tensor_scalar(hn[:, t, :], hn[:, t, :], 0.0, None, ALU.max).then_inc(S("hn4"), 1)
            dve.wait_ge(S("hn4"), NT)
            for t in range(NT):
                dve.wait_ge(S("xin_mm"), t + 1)
                if t >= 2:
                    dve.wait_ge(S(f"st_x{t % 2}"), 32 * (t // 2))
                for h in range(2):
                    link(dve.tensor_copy(out=xst[:, t % 2, h, :, :],
                                         in_=PS[:, XB(t), :].rearrange("p (j h f) -> p h j f", j=4, h=2)[:, h, :, :]))
                dve.sem_inc(S("x_rows"), 1)

            for half in range(2):
                chain = LoopChain(dve, f"l1_chain{half}", 4 * 5)
                base = half * 2 * QUADS

                def products(n, q, i):
                        w = q % 2
                        pr = n + base
                        c = n * 2
                        g = (q + base) % 4
                        xv = xg[:, g, :, 1:4, :]
                        xs = xg[:, g, :, 0, :]
                        uu = slots1[:, ds(c, 2), 3:6].unsqueeze(3).to_broadcast([P, 2, 3, HF])
                        W = PS[:, 5 + w, :].rearrange("p (u b f) -> p u b f", u=2, b=4)
                        dve.wait_ge(S("agg1_mm"), pr + 1)
                        for u in range(2):
                            dve.tensor_scalar(O[:, 2 * w + u, :], iota_n[:, :], local[:, 1, ds(c + u, 1)],
                                              slots1[:, ds(c + u, 1), 2], ALU.is_equal, ALU.mult)
                        dve.wait_ge(S(f"x_in{g}"), i * 32 + 32 + 32 * len(range(g, base, 4)))
                        chain(dve.tensor_tensor(out=xvu, in0=xv, in1=uu, op=ALU.mult))
                        chain(dve.tensor_tensor(out=dotu, in0=xvu[:, :, 0, :], in1=xvu[:, :, 1, :], op=ALU.add))
                        chain(dve.tensor_tensor(out=dotu, in0=dotu, in1=xvu[:, :, 2, :], op=ALU.add))
                        dve.wait_ge(S("w_mm"), pr + 3)
                        chain(dve.tensor_tensor(out=M[:, w, :, 0:2, :], in0=W[:, :, 0:2, :],
                                                in1=xs.unsqueeze(2).to_broadcast([P, 2, 2, HF]), op=ALU.mult))
                        dve.tensor_tensor(out=M[:, w, :, 2, :], in0=W[:, :, 2, :], in1=dotu, op=ALU.mult)
                        dve.tensor_tensor(out=M[:, w, :, 3:6, :],
                                          in0=W[:, :, 3, :].unsqueeze(2).to_broadcast([P, 2, 3, HF]), in1=xv, op=ALU.mult)
                        chain(dve.tensor_tensor(out=M[:, w, :, 6:9, :],
                                                in0=M[:, w, :, 0, :].unsqueeze(2).to_broadcast([P, 2, 3, HF]),
                                                in1=uu, op=ALU.mult))
                        dve.sem_inc(S("m_done"), 1)

                with dve.Fori(0, 2 * QUADS // 4) as i:
                    chain.turn(i)
                    for q in range(4):
                        products(i * 4 + q, q, i)
                chain.turn(2 * QUADS // 4)
                for n in range(2 * QUADS // 4 * 4, 2 * QUADS):
                    products(n, n % 4, n // 4)
                dve.wait_ge(S("agg1_closed"), half + 1)
                for t in range(NT):
                    link(dve.tensor_copy(out=agg1[:, t, :, HF * half:HF * (half + 1)],
                                         in_=PS[:, t, :].rearrange("p (m f) -> p m f", m=NCOMP)))
                dve.sem_inc(S("agg1_sb"), 1)

            dve.wait_ge(S("sz"), 1)
            dve.scalar_tensor_tensor(out=s_e[:, :], in0=s_z[:, :], scalar=-1.0, in1=s_z[:, :],
                                     op0=ALU.mult, op1=ALU.min).then_inc(S("s_abs"), 1)
            link(dve.tensor_scalar(s_z[:, :], s_z[:, :], 0.0, -LOG2, ALU.max, ALU.add))
            dve.wait_ge(S("s_ln"), 1)
            dve.tensor_tensor(out=s_z[:, :], in0=s_z[:, :], in1=s_e[:, :], op=ALU.add).then_inc(S("s_sb"), 1)
            for t in range(NT):
                dve.wait_ge(S("out_mm"), t + 1)
                link(dve.scalar_tensor_tensor(out=X[:, t, 0:C], in0=PS[:, OB(t), 0:C], scalar=RC, in1=X[:, t, 0:C],
                                              op0=ALU.mult, op1=ALU.add))
                xv_out = X[:, t, C:D].rearrange("p (d i) -> p i d", i=3)
                link(dve.scalar_tensor_tensor(out=xv_out, in0=PS[:, OB(t), C:D].rearrange("p (i d) -> p i d", i=3),
                                              scalar=RC, in1=xv_out, op0=ALU.mult, op1=ALU.add))
                dve.sem_inc(S("out_rows"), 1)

        @block.tensor
        def _(pe):
            pe.wait_ge(S("consts"), 7)

            def bucket_sums(k):
                pe.wait_ge(S("counts"), k + 1)
                pe.matmul(PS[:, 0, 0:NT], tri[0:EP, :], cum[:, :, EC - 1], start=True, stop=True)
                pe.matmul(PS[:, 0, NT:2 * NT], ones[0:EP, :], cum[:, :, EC - 1], start=True, stop=True
                          ).then_inc(S("prefix"), 1)

            bucket_sums(0)

            def transposes(groups, ready, done, freed, src, banks):
                pe.wait_ge(S(ready), NT)
                for k in range(groups):
                    if k >= 2:
                        pe.wait_ge(S(freed), k - 1)
                    for t in range(NT):
                        ins = pe.transpose(pair(banks[k % 2])[:, t * P:(t + 1) * P], src(k, t), ident[:, :])
                    ins.then_inc(S(done), 1)

            transposes(KT, "hn1", "t1_ps", "ht1", lambda k, t: hn[:, t, k * P:(k + 1) * P], (0, 2))
            pe.wait_ge(S("ht1"), KT)
            bucket_sums(1)
            pe.wait_ge(S("ld_wqkv"), 16)
            for t in range(NT):
                for j in range(3):
                    n = 3 * t + j
                    if n >= 4:
                        pe.wait_ge(S("qkv_sb"), n - 3)
                    for k in range(KT):
                        ins = pe.matmul(PS[:, 4 + n % 4, :], ht[:, k, t * P:(t + 1) * P], wqkv[:, k, j * D:(j + 1) * D],
                                        start=(k == 0), stop=(k == KT - 1))
                    ins.then_inc(S("qkv_mm"), 1)

            def one_hot_t(c, u):
                pe.wait_ge(S("oh_done"), c + 1)
                pe.wait_ge(S("ot_b"), c + 1)
                pe.transpose(PS[:, 7, 0:P], O[:, u, :], ident[:, :]).then_inc(S("ot_ps"), 1)

            def mask_transposes(c, u):
                pe.wait_ge(S("mask_done"), c + 3)
                pe.wait_ge(S("mask_done_a"), c + 3)
                pe.wait_ge(S("max_done"), c + 1)
                for h in range(H):
                    ins = pe.transpose(pair(2 * u)[:, h * P:(h + 1) * P], masked[:, u, h, :], ident[:, :])
                ins.then_inc(S("mask_t"), 1)

            def k_gather(c, u):
                tile = pe.value_load(tilei[0:1, 0, ds(c, 1)], min_val=0, max_val=NT - 1)
                pe.wait_ge(S("ot_f"), c + 1)
                pe.wait_ge(S("prod_done"), c + 1)
                pe.matmul(PS[:, 4 + u, :], OTf[:, u, :], K_sb[:, ds(tile, 1), :].rearrange("p a n -> p (a n)"),
                          start=True, stop=True).then_inc(S("kg_mm"), 1)

            pe.wait_ge(S("qkv_sb"), 3 * NT)
            pe.wait_ge(S("slots_ready"), 1)
            pe.wait_ge(S("tiles"), 1)
            def first_pass(c, v, i):
                u = v % 2
                if within(c, ahead=1):
                    one_hot_t(c + 1, 1 - u)
                if within(c, back=1):
                    mask_transposes(c - 1, 1 - u)
                if within(c, ahead=1):
                    k_gather(c + 1, 1 - u)

            one_hot_t(0, 0)
            k_gather(0, 0)
            quads(pe, first_pass)
            mask_transposes(CH - 1, 1)

            pe.wait_ge(S("mc_done"), 1)
            pe.wait_ge(S("ot_b"), CH + 1)
            for b in range(CH // QB):
                with pe.Fori(0, QB) as j:
                    pe.matmul(PS[:, b, ds(j * 3 * H, 3 * H)], OTb[:, ds((j + b * QB) * P, P)],
                              mc3[:, ds(j + b * QB, 1), :, :].rearrange("p c a h -> p (c a h)"),
                              start=True, stop=True).then_inc(S("mx_mm"), 1)

            def open_close(banks, start):
                for b in banks:
                    ins = pe.matmul(PS[:, b, :], zeros_l, zeros_r, start=start, stop=not start)
                return ins

            zeros_l, zeros_r = zero_w[:, 0:P], zero_w[:, :]
            pe.wait_ge(S("shifted"), 1)
            open_close(range(6), True)

            def second_pass(c, v, i):
                u = v % 2
                tile = pe.value_load(tilei[0:1, 0, ds(c, 1)], min_val=0, max_val=NT - 1)
                pe.wait_ge(S("msg_done"), c + 3)
                pe.matmul(PS[:, ds(tile, 1), :].rearrange("p a n -> p (a n)"), O[:, u, :], msg[:, u, :],
                          start=False, stop=False)
                pe.matmul(PS[:, 5, ds(tile * H, H)], O[:, u, :],
                          logit[:, ds(c, 1), :].rearrange("p a h -> p (a h)"),
                          start=False, stop=False).then_inc(S("agg_mm"), 1)

            quads(pe, second_pass)
            open_close(range(6), False).then_inc(S("agg_closed"), 1)

            pe.wait_ge(S("att_sb"), NT)
            transposes(KT, "att_sb", "t2_ps", "ht2", lambda k, t: hn[:, t, k * P:(k + 1) * P], (4, 6))
            pe.wait_ge(S("ht2"), KT)
            pe.wait_ge(S("ld_wo"), 16)
            for t in range(NT):
                if t >= 4:
                    pe.wait_ge(S("h1_sb"), t - 3)
                for k in range(KT):
                    ins = pe.matmul(PS[:, t % 4, :], ht[:, k, t * P:(t + 1) * P], WO[:, k, :],
                                    start=(k == 0), stop=(k == KT - 1))
                ins.then_inc(S("wo_mm"), 1)
            pe.wait_ge(S("h1_sb"), NT)
            transposes(KT, "hn3", "t3_ps", "ht3", lambda k, t: hn[:, t, k * P:(k + 1) * P], (0, 2))
            pe.wait_ge(S("ht3"), KT)
            pe.wait_ge(S("ld_w1"), 16)
            for f in range(FT):
                if f >= 2:
                    pe.wait_ge(S("gelu"), f - 1)
                for a in range(2):
                    for k in range(KT):
                        ins = pe.matmul(PS[:, 4 + 2 * (f % 2) + a, 0:NH], w1[:, k, f * P:(f + 1) * P],
                                        ht[:, k, a * NH:(a + 1) * NH], start=(k == 0), stop=(k == KT - 1))
                ins.then_inc(S("w1_mm"), 1)
            def filter_rows(g):
                r = g % 2
                if g >= 2:
                    pe.wait_ge(S("ft_sb"), g - 1)
                for a in range(G4):
                    ins = pe.transpose(PS[0:NRBF, 4 + r, a * P:(a + 1) * P], slots1[:, g * G4 + a, 6:W1], ident[:, :])
                ins.then_inc(S("ft_t"), 1)

            def filter_hidden(g):
                r = g % 2
                pe.wait_ge(S("ft_sb"), g + 1)
                if g >= 2:
                    pe.wait_ge(S("z_sb"), g - 1)
                pe.matmul(PS[:, 6 + r, :], wf1[:, :], ft[0:NRBF, r, :], start=True, stop=True).then_inc(S("z_mm"), 1)

            pe.wait_ge(S("gelu"), FT)
            pe.wait_ge(S("ld_w2a"), 16)
            pe.wait_ge(S("ld_slots1"), 16)
            pe.wait_ge(S("ld_l1"), 16 * 8)
            pe.wait_ge(S("ld_w2b"), 16)
            filter_rows(0)
            step = 0
            for t in range(NT):
                if t >= 4:
                    pe.wait_ge(S("x1_sb"), t - 3)
                for f in range(FT):
                    ins = pe.matmul(PS[:, t % 4, :], gelu_t[:, f, t * P:(t + 1) * P], w2[:, f, :],
                                    start=(f == 0), stop=(f == FT - 1))
                    if f == FT - 1:
                        ins.then_inc(S("w2_mm"), 1)
                    if f % 4 == 1 and step + 1 < CH // G4:
                        filter_rows(step + 1)
                    if f % 4 == 3:
                        filter_hidden(step)
                        step += 1
            while step < CH // G4:
                filter_hidden(step)
                step += 1

            pe.wait_ge(S("x1_sb"), NT)
            transposes(4, "hn4", "t4_ps", "ht4",
                       lambda j, t: hn[:, t, 0:C] if j == 0 else hn[:, t, C + j - 1:D:3], (0, 2))
            pe.wait_ge(S("ht4"), 4)
            pe.wait_ge(S("ld_l1"), 16 * 8)
            for t in range(NT):
                for j in range(4):
                    ins = pe.matmul(PS[:, XB(t), j * C:(j + 1) * C], xin_t[:, j, t * P:(t + 1) * P],
                                    win[:, min(j, 1), :], start=True, stop=True)
                ins.then_inc(S("xin_mm"), 1)

            pe.wait_ge(S("x_rows"), NT)
            pe.wait_ge(S("h_done"), CH // G4)
            pe.wait_ge(S("tiles"), 2)

            def filters(i, w, half):
                pr = i * 2 + w + half * 2 * QUADS
                pe.wait_ge(S("hs_done"), pr + 1)
                pe.wait_ge(S("m_done"), pr + 1)
                for u in range(2):
                    dst = PS[:, 5 + w, u * 4 * HF:(u + 1) * 4 * HF]
                    pe.matmul(dst, hs[:, w, u * P:(u + 1) * P], wf2[:, half, :], start=True, stop=False)
                    ins = pe.matmul(dst, ones[0:1, :], bf2[:, half, :], start=False, stop=True)
                ins.then_inc(S("w_mm"), 1)

            def scatter(i, w, half):
                pr = i * 2 + w + half * 2 * QUADS
                tiles = [pe.value_load(tilei[0:1, 1, ds(i * 4 + 2 * w + u, 1)], min_val=0, max_val=NT - 1)
                         for u in range(2)]
                pe.wait_ge(S("m_done"), pr + 3)
                for u in range(2):
                    ins = pe.matmul(PS[:, ds(tiles[u], 1), :].rearrange("p a n -> p (a n)"), O[:, 2 * w + u, :],
                                    M[:, w, u, 1:9, :].rearrange("p m f -> p (m f)"), start=False, stop=False)
                ins.then_inc(S("agg1_mm"), 1)

            for half in range(2):
                if half:
                    pe.wait_ge(S("agg1_sb"), half)
                open_close(range(NT), True)
                filters(0, 0, half)
                with pe.Fori(0, QUADS - 1) as i:
                    filters(i, 1, half)
                    scatter(i, 0, half)
                    filters(i + 1, 0, half)
                    scatter(i, 1, half)
                filters(QUADS - 1, 1, half)
                scatter(QUADS - 1, 0, half)
                scatter(QUADS - 1, 1, half)
                open_close(range(NT), False).then_inc(S("agg1_closed"), 1)

            pe.wait_ge(S("agg1_sb"), 2)
            for m in range(NCOMP):
                if m >= 2:
                    pe.wait_ge(S("at_sb"), m - 1)
                for t in range(NT):
                    ins = pe.transpose(pair(2 * (m % 2))[:, t * P:(t + 1) * P], agg1[:, t, m, :], ident[:, :])
                ins.then_inc(S("t5_ps"), 1)
            pe.wait_ge(S("at_sb"), NCOMP)
            for a in range(2):
                for k in range(2):
                    ins = pe.matmul(PS[:, 4 + a, 0:NH], w1sv[:, 0, k, :], agg_t[:, k, a * NH:(a + 1) * NH],
                                    start=(k == 0), stop=(k == 1))
            ins.then_inc(S("s_mm"), 1)
            for i in range(3):
                if i == 2:
                    pe.wait_ge(S("v_sb"), 1)
                b = 6 if i % 2 == 0 else 0
                for a in range(2):
                    for k in range(2):
                        ins = pe.matmul(PS[:, b + a, 0:NH], w1sv[:, 1, k, :], agg_t[:, (5 if k == 0 else 2) + i, a * NH:(a + 1) * NH],
                                        start=(k == 0), stop=(k == 1))
                ins.then_inc(S("v_mm"), 1)
            pe.wait_ge(S("v_sb"), 3)
            pe.wait_ge(S("s_sb"), 1)
            for t in range(NT):
                for j in range(4):
                    lhs = s_z if j == 0 else v_t[:, j - 1, :]
                    ins = pe.matmul(PS[:, OB(t), j * C:(j + 1) * C], lhs[:, t * P:(t + 1) * P], w2sv[:, min(j, 1), :],
                                    start=True, stop=True)
                ins.then_inc(S("out_mm"), 1)


_OUTS = [((625, 512), "float32")]


def kernel(**inputs):
    import numpy as _np
    import concourse.bacc as _bacc
    from concourse import mybir as _mybir
    from concourse.bass_utils import run_bass_kernel_spmd as _run

    nc = _bacc.Bacc("TRN2", target_bir_lowering=False, num_devices=1)
    arrays, args = {}, {}
    for name in inputs:
        a = _np.ascontiguousarray(inputs[name])
        arrays[f"in_{name}_dram"] = a
        args[name] = nc.dram_tensor(f"in_{name}_dram", a.shape, _mybir.dt.from_np(a.dtype), kind="ExternalInput").ap()
    out = nc.dram_tensor("out_0_dram", _OUTS[0][0], _mybir.dt.from_np(_np.dtype(_OUTS[0][1])), kind="ExternalOutput").ap()
    gnn_two_layer_kernel(nc, args, out)
    r = _run(nc, [arrays], core_ids=[0])
    return r.results[0]["out_0_dram"]
```
